# Optimizing a Trainium2 kernel written in Bass

```python
import numpy as np
import jax
import jax.numpy as jnp

def _softmax(x, axis=-1):
    return jax.nn.softmax(x, axis=axis)

def _gelu(x):
    return jax.nn.gelu(x, approximate=True)

def _silu(x):
    return jax.nn.silu(x)

def _sigmoid(x):
    return jax.nn.sigmoid(x)

def _layernorm(x, axis=-1, eps=1e-05):
    m = jnp.mean(x, axis=axis, keepdims=True)
    v = jnp.var(x, axis=axis, keepdims=True)
    return (x - m) / jnp.sqrt(v + eps)

def _scatter_add(tgt, idx, src, axis=0):
    return tgt.at[idx].add(src)

def _segment_sum(src, seg, n):
    return jax.ops.segment_sum(src, seg, n)
kernel_name = 'mk_cond_resid_d4_seqx_r8_bac54e'

def setup_inputs(seed: int=0):
    np.random.seed(seed)
    _w = jnp.asarray

    def _rec_inputs():
        import jax
        import jax.numpy as jnp
        _rk = jax.random.key(seed)
        x = -0.000125 + 0.9999 * jax.random.normal(jax.random.fold_in(_rk, 1), (8, 128, 512), jnp.float32)
        _lenS = 128 - jax.random.randint(jax.random.fold_in(_rk, 7), (8,), 0, max(1, 128 // 4) + 1, jnp.int32)
        _lenS2 = 128 - jax.random.randint(jax.random.fold_in(_rk, 8), (8,), 0, max(1, 128 // 4) + 1, jnp.int32)
        itok_B_0_7 = jax.random.randint(jax.random.fold_in(_rk, 11), (8,), 0, 8, jnp.int32)
        itok_B_1_7 = jax.random.randint(jax.random.fold_in(_rk, 12), (8,), 1, 8, jnp.int32)
        itok_B_6_15 = jax.random.randint(jax.random.fold_in(_rk, 13), (8,), 6, 16, jnp.int32)
        itok_B_3_7 = jax.random.randint(jax.random.fold_in(_rk, 14), (8,), 3, 8, jnp.int32)
        return (x, itok_B_0_7, itok_B_1_7, itok_B_6_15, itok_B_3_7)
    x, itok_B_0_7, itok_B_1_7, itok_B_6_15, itok_B_3_7 = _rec_inputs()

    def _L0_cond_setup():
        import jax, jax.numpy as jnp
        import numpy as np
        TOP_K = 2
        LANG_BIAS = 5.0
        SCALING = 32.0 / 16.0
        LANGUAGE_PAD_ID = -1
        key = jax.random.key(seed)
        ks = jax.random.split(key, 6)
        B, T, D, O, E, R = (4, 256, 512, 512, 8, 16)
        x = jax.random.normal(ks[0], (B, T, D), dtype=jnp.float32)
        language_ids = jax.random.randint(ks[1], (B,), 0, E).astype(jnp.int64)
        W = jax.random.normal(ks[2], (O, D), dtype=jnp.float32) * (1.0 / np.sqrt(D))
        Wr = jax.random.normal(ks[3], (E, D), dtype=jnp.float32) * (1.0 / np.sqrt(D))
        A = jax.random.normal(ks[4], (E, R, D), dtype=jnp.float32) * (1.0 / np.sqrt(D))
        Bm = jax.random.normal(ks[5], (O, R), dtype=jnp.float32) * 0.0
        Bm = jnp.broadcast_to(Bm, (E, O, R)) + jax.random.normal(ks[5], (E, O, R), dtype=jnp.float32) * 0.02
        return {'x': x, 'language_ids': language_ids, 'W': W, 'Wr': Wr, 'A': A, 'B': Bm}
    _L0_cond_all = _L0_cond_setup()
    _L0_cond_in = {k: v for k, v in _L0_cond_all.items() if k in ('W', 'Wr', 'A', 'B')}
    del _L0_cond_all

    def _L1_cond_setup():
        import jax, jax.numpy as jnp
        import numpy as np
        B, S, D_IN, D_OUT = (4, 256, 512, 512)
        N_ADAPTERS, MAX_RANK = (8, 16)
        key = jax.random.key(seed)
        ks = jax.random.split(key, 7)
        x = jax.random.normal(ks[0], (B, S, D_IN), dtype=jnp.float32)
        weight = jax.random.normal(ks[1], (D_OUT, D_IN), dtype=jnp.float32) * (1.0 / np.sqrt(D_IN))
        bias = jax.random.normal(ks[2], (D_OUT,), dtype=jnp.float32) * 0.01
        lora_a_weights = jax.random.normal(ks[3], (N_ADAPTERS, MAX_RANK, D_IN), dtype=jnp.float32) * (1.0 / np.sqrt(D_IN))
        lora_b_weights = jax.random.normal(ks[4], (N_ADAPTERS, D_OUT, MAX_RANK), dtype=jnp.float32) * 0.02
        scaling_factors = jax.random.uniform(ks[5], (N_ADAPTERS,), dtype=jnp.float32, minval=0.5, maxval=2.0)
        adapter_id = jax.random.randint(ks[6], (B,), 0, N_ADAPTERS, dtype=jnp.int64)
        return {'x': x, 'weight': weight, 'bias': bias, 'lora_a_weights': lora_a_weights, 'lora_b_weights': lora_b_weights, 'scaling_factors': scaling_factors, 'adapter_id': adapter_id}
    _L1_cond_all = _L1_cond_setup()
    _L1_cond_in = {k: v for k, v in _L1_cond_all.items() if k in ('weight', 'bias', 'lora_a_weights', 'lora_b_weights', 'scaling_factors')}
    del _L1_cond_all

    def _L2_cond_setup():
        import jax, jax.numpy as jnp
        import numpy as np
        B, S, D_IN, D_OUT = (4, 256, 512, 512)
        RANK, MAX_LORAS = (16, 32)
        key = jax.random.key(seed)
        ks = jax.random.split(key, 6)
        x = jax.random.normal(ks[0], (B, S, D_IN), dtype=jnp.float32)
        adapter_ids = jax.random.randint(ks[1], (B,), 0, MAX_LORAS)
        base_weight = jax.random.normal(ks[2], (D_OUT, D_IN), dtype=jnp.float32) * D_IN ** (-0.5)
        base_bias = jax.random.normal(ks[3], (D_OUT,), dtype=jnp.float32) * 0.01
        lora_A_w = jax.random.normal(ks[4], (MAX_LORAS, RANK, D_IN), dtype=jnp.float32) * D_IN ** (-0.5)
        lora_B_w = jax.random.normal(ks[5], (MAX_LORAS, D_OUT, RANK), dtype=jnp.float32) * RANK ** (-0.5)
        return {'x': x, 'adapter_ids': adapter_ids, 'base_weight': base_weight, 'base_bias': base_bias, 'lora_A_w': lora_A_w, 'lora_B_w': lora_B_w}
    _L2_cond_all = _L2_cond_setup()
    _L2_cond_in = {k: v for k, v in _L2_cond_all.items() if k in ('base_weight', 'base_bias', 'lora_A_w', 'lora_B_w')}
    del _L2_cond_all

    def _L3_cond_setup():
        import jax, jax.numpy as jnp
        import numpy as np
        MAX_LORAS, OUT, IN = (8, 512, 512)
        B, S = (4, 256)
        key = jax.random.key(seed)
        k1, k2, k3 = jax.random.split(key, 3)
        x = jax.random.normal(k1, (B, S, IN), dtype=jnp.float32)
        weight = jax.random.normal(k2, (MAX_LORAS, OUT, IN), dtype=jnp.float32) * 0.02
        adapter_ids = jax.random.randint(k3, (B,), 0, MAX_LORAS, dtype=jnp.int32)
        return {'x': x, 'weight': weight, 'adapter_ids': adapter_ids}
    _L3_cond_all = _L3_cond_setup()
    _L3_cond_in = {k: v for k, v in _L3_cond_all.items() if k in ('weight',)}
    del _L3_cond_all
    return {'x': x, 'itok_B_0_7': itok_B_0_7, 'itok_B_1_7': itok_B_1_7, 'itok_B_6_15': itok_B_6_15, 'itok_B_3_7': itok_B_3_7, 'L0_cond_W': _L0_cond_in['W'], 'L0_cond_Wr': _L0_cond_in['Wr'], 'L0_cond_A': _L0_cond_in['A'], 'L0_cond_B': _L0_cond_in['B'], 'L1_cond_weight': _L1_cond_in['weight'], 'L1_cond_bias': _L1_cond_in['bias'], 'L1_cond_lora_a_weights': _L1_cond_in['lora_a_weights'], 'L1_cond_lora_b_weights': _L1_cond_in['lora_b_weights'], 'L1_cond_scaling_factors': _L1_cond_in['scaling_factors'], 'L2_cond_base_weight': _L2_cond_in['base_weight'], 'L2_cond_base_bias': _L2_cond_in['base_bias'], 'L2_cond_lora_A_w': _L2_cond_in['lora_A_w'], 'L2_cond_lora_B_w': _L2_cond_in['lora_B_w'], 'L3_cond_weight': _L3_cond_in['weight']}

def reference(x, itok_B_0_7, itok_B_1_7, itok_B_6_15, itok_B_3_7, L0_cond_W, L0_cond_Wr, L0_cond_A, L0_cond_B, L1_cond_weight, L1_cond_bias, L1_cond_lora_a_weights, L1_cond_lora_b_weights, L1_cond_scaling_factors, L2_cond_base_weight, L2_cond_base_bias, L2_cond_lora_A_w, L2_cond_lora_B_w, L3_cond_weight):
    import jax
    import jax.numpy as jnp

    def _L0_cond_ref(x, language_ids, W, Wr, A, B):
        import jax, jax.numpy as jnp
        import numpy as np
        TOP_K = 2
        LANG_BIAS = 5.0
        SCALING = 32.0 / 16.0
        LANGUAGE_PAD_ID = -1
        base = jnp.einsum('btd,od->bto', x, W)
        E = Wr.shape[0]
        logits = jnp.einsum('btd,ed->bte', x.astype(jnp.float32), Wr.astype(jnp.float32))
        expert_targets = language_ids
        valid = expert_targets >= 0
        tgt = jnp.where(valid, expert_targets, 0)
        bias = jax.nn.one_hot(tgt, E, dtype=logits.dtype) * LANG_BIAS
        bias = jnp.where(valid[:, None], bias, 0.0)
        logits = logits + bias[:, None, :]
        topw, topi = jax.lax.top_k(logits, TOP_K)
        weights = jax.nn.softmax(topw, axis=-1)
        gates = jnp.sum(jax.nn.one_hot(topi, E, dtype=weights.dtype) * weights[..., None], axis=-2)
        gates = gates.astype(x.dtype)
        h = jnp.einsum('btd,erd->bter', x, A)
        lora_out = jnp.einsum('bter,bte,eor->bto', h, gates, B)
        return base + SCALING * lora_out

    def _L1_cond_ref(x, weight, bias, lora_a_weights, lora_b_weights, scaling_factors, adapter_id):
        import jax, jax.numpy as jnp
        import numpy as np
        B, S, D_IN, D_OUT = (4, 256, 512, 512)
        N_ADAPTERS, MAX_RANK = (8, 16)
        base = jnp.einsum('bsi,oi->bso', x, weight) + bias
        a_sel = lora_a_weights[adapter_id]
        b_sel = lora_b_weights[adapter_id]
        scale = scaling_factors[adapter_id]
        low = jnp.einsum('bsi,bri->bsr', x, a_sel)
        delta = jnp.einsum('bsr,bor->bso', low, b_sel)
        return base + scale[:, None, None] * delta

    def _L2_cond_ref(x, adapter_ids, base_weight, base_bias, lora_A_w, lora_B_w):
        import jax, jax.numpy as jnp
        import numpy as np
        B, S, D_IN, D_OUT = (4, 256, 512, 512)
        RANK, MAX_LORAS = (16, 32)
        result = jnp.einsum('bsd,od->bso', x, base_weight) + base_bias
        A = lora_A_w[adapter_ids]
        Bw = lora_B_w[adapter_ids]
        h = jnp.einsum('bsd,brd->bsr', x, A)
        lora_out = jnp.einsum('bsr,bor->bso', h, Bw)
        result = result + lora_out
        return result.astype(x.dtype)

    def _L3_cond_ref(x, weight, adapter_ids):
        import jax, jax.numpy as jnp
        import numpy as np
        MAX_LORAS, OUT, IN = (8, 512, 512)
        B, S = (4, 256)
        w = weight[adapter_ids]
        return jnp.einsum('bsi,boi->bso', x, w)
    x = x + _L0_cond_ref(x, itok_B_0_7, L0_cond_W, L0_cond_Wr, L0_cond_A, L0_cond_B)
    x = x + _L1_cond_ref(x, L1_cond_weight, L1_cond_bias, L1_cond_lora_a_weights, L1_cond_lora_b_weights, L1_cond_scaling_factors, itok_B_1_7)
    x = x + _L2_cond_ref(x, itok_B_6_15, L2_cond_base_weight, L2_cond_base_bias, L2_cond_lora_A_w, L2_cond_lora_B_w)
    x = x + _L3_cond_ref(x, L3_cond_weight, itok_B_3_7)
    return x

_drawn_inputs = setup_inputs


def setup_inputs(seed=0):
    import zlib

    import numpy as np

    out = dict(_drawn_inputs(seed))
    spreads = {}
    factors = {'L0_cond_Wr': 6.086,
     'L1_cond_bias': 8.0,
     'L1_cond_scaling_factors': 3.155,
     'L2_cond_base_bias': 24.62}
    for name, (base, spread) in spreads.items():
        noise = np.random.default_rng([zlib.crc32(name.encode()), seed]).standard_normal(out[name].shape)
        drawn = base * np.exp(spread * noise) if base else spread * noise
        out[name] = jnp.asarray(drawn.astype(out[name].dtype))
    for name, factor in factors.items():
        out[name] = (out[name] * factor).astype(out[name].dtype)
    return out
```

```python
from contextlib import ExitStack

import concourse.bass as bass
from concourse import mybir

F32 = mybir.dt.float32
F32R = mybir.dt.float32r
I32 = mybir.dt.int32
ALU = mybir.AluOpType
ACT = mybir.ActivationFunctionType
AX_X = mybir.AxisListType.X

P = 128
NB, T, D = 8, 128, 512
NK = D // P
NG = 2
GB = NB // NG
GT = GB * T
NE, R = 8, 16
N2 = 32
PAIRS = NB // 2
PW = 2 * R
PT = 2 * T
LANG_BIAS = 5.0
SCALING = 2.0

C_IDENT, C_EXPERT, C_TIE, C_OWN = 0, P, P + NE, P + NE + NE * NE
C_ALL = C_OWN + NB

RAW_SLOTS = 3
ENTRIES = ["x g0", "W0", "low0", "x g1", "B1", "W1", "W2", "B2"] + [f"W3 b{b}" for b in range(NB)]
W_SETS = 4
STAGES = 4


def entry(name):
    return ENTRIES.index(name)


def slot(name):
    return entry(name) % RAW_SLOTS


def loaded_before(name):
    return entry(name) // RAW_SLOTS


def build(nc, x_t, w_t, w3_t, a0_t, b0_t, a1_t, b1_t, a2_t, b2_t, bias1, bias2, scale1,
          id0, id1, id2, id3, consts, out):
    with ExitStack() as ctx:
        def sb(name, shape, dt):
            return ctx.enter_context(nc.sbuf_tensor(name, shape, dt))

        def ps(name, shape):
            return ctx.enter_context(nc.psum_tensor(name, shape, F32))

        def sem(name):
            return ctx.enter_context(nc.semaphore(name))

        raw = sb("raw", [P, RAW_SLOTS, NK * D], F32)
        x_hi = [sb(f"x_hi{i}", [P, NK, NB * T], F32R) for i in range(2)]
        x_lo = [sb(f"x_lo{i}", [P, NK, NB * T], F32R) for i in range(2)]
        w_hi = [sb(f"w_hi{i}", [P, NK, D], F32R) for i in range(W_SETS)]
        w_lo = [sb(f"w_lo{i}", [P, NK, D], F32R) for i in range(W_SETS)]
        a0_hi, a0_lo = sb("a0_hi", [P, NK, NE * R], F32R), sb("a0_lo", [P, NK, NE * R], F32R)
        b0_hi, b0_lo = sb("b0_hi", [P, D], F32R), sb("b0_lo", [P, D], F32R)
        router = sb("router", [P, NK, 2 * NE], F32R)
        a_raw = sb("a_raw", [P, NB, NK, R], F32)
        a_stat = sb("a_stat", [P, PAIRS, NK, P], F32R)
        b_stat = [sb(f"b_stat{i}", [P, PAIRS, D], F32R) for i in range(2)]
        ranks = sb("ranks", [P, 2, GT], F32R)
        stage = sb("stage", [P, STAGES, D], F32)
        beats, ties = (stage[:, 0, i * GB * NE * NE:(i + 1) * GB * NE * NE]
                       .rearrange("p (b i j) -> p b i j", b=GB, i=NE) for i in range(2))
        gate_t, gated = stage[:, 1, :], stage[:, 2, :]
        gate_wide = stage[:, 3, :].rearrange("p (b e r) -> p b e r", b=GB, e=NE)
        const = sb("const", [P, C_ALL], F32)
        ids = sb("ids", [1, 3, NB], I32)
        ids_all = sb("ids_all", [P, 2, NB], I32)
        ids_f = sb("ids_f", [P, 2, NB], F32)
        scale_all = sb("scale_all", [P, NE], F32)
        bias = sb("bias", [P, 2, NK], F32)
        lang = sb("lang", [P, NB, NE], F32)
        pick = sb("pick", [P, NB, NE], F32)
        scale_b = sb("scale_b", [P, NB], F32)
        own_scaled = sb("own_scaled", [P, NB], F32)
        logits = sb("logits", [P, GB, NE], F32)
        top = sb("top", [P, GB], F32)
        rank = sb("rank", [P, GB, NE], F32)
        shifted = sb("shifted", [P, GB, NE], F32)
        expd = sb("expd", [P, GB, NE], F32)
        kept = sb("kept", [P, GB, NE], F32)
        total = sb("total", [P, GB], F32)
        gates = sb("gates", [P, GB, NE], F32)

        ident = const[:, C_IDENT:C_IDENT + P]
        expert = const[:, C_EXPERT:C_EXPERT + NE]
        tie = const[:, C_TIE:C_TIE + NE * NE].rearrange("p (i j) -> p i j", i=NE)
        own = const[:, C_OWN:C_OWN + NB]

        acc = [ps(f"acc{i}", [P, D]) for i in range(4)]
        low = [ps(f"low{i}", [P, GT]) for i in range(2)]
        logit_ps = ps("logit_ps", [P, NB, 2, NE])
        gate_ps = ps("gate_ps", [P, GT])

        consts_in = sem("consts_in")
        small_in = sem("small_in")
        ids_in = sem("ids_in")
        x0_in = [sem(f"x0_in{k}") for k in range(NK)]
        w0_in = [sem(f"w0_in{k}") for k in range(NK)]
        low0_in = [sem(f"low0_in{i}") for i in range(2)]
        raw_in = [sem(f"raw_in{i}") for i in range(RAW_SLOTS)]
        a_in = sem("a_in")
        masks_made = sem("masks_made")
        eye_added = sem("eye_added")
        w_hi_made = sem("w_hi_made")
        w_made = sem("w_made")
        x_hi_made = sem("x_hi_made")
        x_made = sem("x_made")
        low0_hi_made = sem("low0_hi_made")
        low0_made = sem("low0_made")
        a_hi_made = sem("a_hi_made")
        a_copied = sem("a_copied")
        a_made = sem("a_made")
        b_hi_made = sem("b_hi_made")
        b_made = sem("b_made")
        logits_done = sem("logits_done")
        logits_read = sem("logits_read")
        dve_step = sem("dve_step")
        shifted_made = sem("shifted_made")
        exp_done = sem("exp_done")
        gates_made = sem("gates_made")
        gates_widened = sem("gates_widened")
        gates_turned = sem("gates_turned")
        gates_copied = sem("gates_copied")
        low_done = sem("low_done")
        gated_made = sem("gated_made")
        ranks_hi_made = sem("ranks_hi_made")
        ranks_made = sem("ranks_made")
        acc_done = sem("acc_done")
        acc_hi_made = sem("acc_hi_made")
        acc_read = sem("acc_read")
        out_read_act = sem("out_read_act")
        out_read_dve = sem("out_read_dve")
        stored = [sem(f"stored{i}") for i in range(STAGES)]

        W_ORDER = ["W0", "W1", "W2"] + [f"W3 b{b}" for b in range(NB)]

        def w_count(name):
            return NK + W_ORDER.index(name)

        def w_set(name):
            return W_ORDER.index(name) % W_SETS

        def bank_no(layer, g, m):
            return (layer * NG + g) * NK + m

        def bank_no_l3(b):
            return 3 * NG * NK + b

        def low_count(layer, pair):
            return NG + (layer - 1) * PAIRS + pair + 1

        def batch_cols(b):
            return slice(b * T, (b + 1) * T)

        def group_cols(g):
            return slice(g * GT, (g + 1) * GT)

        def raw_value(name, half=False):
            dmas = {"x g0": 0, "W0": 0, "low0": 0, "B1": NB * (P // PW), "B2": NB * (P // PW)}
            n = sum(dmas.get(e, 1) for i, e in enumerate(ENTRIES[:entry(name) + 1])
                    if i % RAW_SLOTS == slot(name))
            return 16 * n

        def a_pair(t, pair):
            return t[:, 2 * pair:2 * pair + 2, :, :].rearrange("p s k r -> p k s r")

        def a_group(pair, group):
            return a_stat[:, pair, :, group * PW:(group + 1) * PW].rearrange("p k (s r) -> p k s r", s=2)

        def wait_w_set(eng, name):
            n = W_ORDER.index(name) - W_SETS
            if n >= 0:
                last = bank_no(n, NG - 1, NK - 1) if n < 3 else bank_no_l3(n - 3)
                eng.wait_ge(acc_done, last + 1)

        block = ctx.enter_context(nc.Block())

        @block.sync
        def _(sp):
            def free_slot(name):
                e = entry(name) - RAW_SLOTS
                if e < 0:
                    return
                old = ENTRIES[e]
                if old == "x g0":
                    sp.wait_ge(x_made, NK)
                elif old == "x g1":
                    sp.wait_ge(x_made, NK + 1)
                elif old == "low0":
                    sp.wait_ge(low0_made, 2)
                elif old[0] == "B":
                    sp.wait_ge(b_made, int(old[1]))
                else:
                    sp.wait_ge(w_made, w_count(old))

            def load(name, src):
                free_slot(name)
                dst = raw[:, slot(name), :].rearrange("p (k n) -> p k n", k=NK)
                sp.dma_start(dst, src).then_inc(raw_in[slot(name)], 16)

            def gather_a(a_dram, which, n):
                with sp.Fori(0, NB) as b:
                    a = sp.value_load(ids[0:1, which, bass.ds(b, 1)], min_val=0, max_val=n - 1)
                    sp.dma_start(a_raw[:, bass.ds(b, 1), :, :].rearrange("p b k r -> p (b k r)"),
                                 a_dram[bass.ds(a, 1)].rearrange("a p n -> p (a n)")).then_inc(a_in, 16)

            def gather_b(b_dram, which, n, name):
                free_slot(name)
                dst = raw[:, slot(name), :].rearrange("p (q n) -> p q n", q=PAIRS)
                with sp.Fori(0, PAIRS) as q:
                    for side in range(2):
                        a = sp.value_load(ids[0:1, which, bass.ds(2 * q + side, 1)],
                                          min_val=0, max_val=n - 1)
                        for group in range(P // PW):
                            row = group * PW + side * R
                            sp.dma_start(dst[row:row + R, bass.ds(q, 1), :].rearrange("p q n -> p (q n)"),
                                         b_dram[bass.ds(a, 1)].rearrange("a r n -> r (a n)"))\
                              .then_inc(raw_in[slot(name)], 16)

            low0 = raw[:, slot("low0"), :]
            sp.dma_start(low0[:, 0:NK * (P + NE)], a0_t).then_inc(low0_in[0], 16)
            for k in range(NK):
                sp.dma_start(raw[:, slot("x g0"), k * GT:(k + 1) * GT], x_t[0, :, k, :])\
                  .then_inc(x0_in[k], 16)
            sp.dma_start(const[:, :], consts).then_inc(consts_in, 16)
            for k in range(NK):
                sp.dma_start(raw[:, slot("W0"), k * D:(k + 1) * D], w_t[0, :, k, :]).then_inc(w0_in[k], 16)
            sp.dma_start(low0[:, NK * (P + NE):NK * (P + NE) + D], b0_t).then_inc(low0_in[1], 16)
            for i, src in enumerate((id1, id2, id3)):
                sp.dma_start(ids[:, i, :], src.rearrange("(a b) -> a b", a=1)).then_inc(ids_in, 16)
            load("x g1", x_t[1])
            sp.wait_ge(ids_in, 3 * 16)
            gather_a(a1_t, 0, NE)
            gather_b(b1_t, 0, NE, "B1")
            load("W1", w_t[1])
            load("W2", w_t[2])
            gather_b(b2_t, 1, N2, "B2")
            sp.wait_ge(a_made, 1)
            gather_a(a2_t, 1, N2)

            def load_w3(b):
                a = sp.value_load(ids[0:1, 2, b:b + 1], min_val=0, max_val=NE - 1)
                load(f"W3 b{b}", w3_t[bass.ds(a, 1)].rearrange("a p k n -> p (a k) n"))

            def store(b):
                sp.wait_ge(out_read_dve if b % 2 else out_read_act, b // 2 + 1)
                sp.dma_start(out[b], stage[:, b % STAGES, :]).then_inc(stored[b % STAGES], 16)

            for b in range(NB - 2):
                load_w3(b)
            load_w3(NB - 2)
            store(0)
            load_w3(NB - 1)
            for b in range(1, NB):
                store(b)
            for i in range(STAGES):
                sp.wait_ge(stored[i], 16 * (NB // STAGES))

        @block.gpsimd
        def _(pool):
            pool.dma_start(ids_all[:, 0, :], id0.rearrange("(a b) -> a b", a=1).to_broadcast([P, NB]))\
                .then_inc(small_in, 16)
            pool.dma_start(ids_all[:, 1, :], id1.rearrange("(a b) -> a b", a=1).to_broadcast([P, NB]))\
                .then_inc(small_in, 16)
            pool.dma_start(scale_all[:, :], scale1.rearrange("(a b) -> a b", a=1).to_broadcast([P, NE]))\
                .then_inc(small_in, 16)
            pool.dma_start(bias[:, 0, :], bias1).then_inc(small_in, 16)
            pool.dma_start(bias[:, 1, :], bias2).then_inc(small_in, 16)
            pool.wait_ge(consts_in, 16)

            def add_eye(name, k):
                block_k = raw[:, slot(name), k * (D + P):k * (D + P) + P]
                return nc.gpsimd.tensor_tensor(block_k, block_k, ident, ALU.add)

            for k in range(NK):
                pool.wait_ge(w0_in[k], 16)
                add_eye("W0", k).then_inc(eye_added, 1)

            def eye(name):
                pool.wait_ge(raw_in[slot(name)], raw_value(name))
                for k in range(NK):
                    ins = add_eye(name, k)
                ins.then_inc(eye_added, 1)

            def copy_a(n):
                pool.wait_ge(a_hi_made, n)
                sets = a_stat[:, :, :, :].rearrange("p q k m -> p (q k) m")
                for group in (1, 3):
                    ins = nc.gpsimd.tensor_copy(sets[:, :, group * PW:(group + 1) * PW],
                                                sets[:, :, 0:PW].bitcast(F32))
                ins.then_inc(a_copied, 1)

            copy_a(1)
            eye("W1")
            eye("W2")
            eye("W3 b0")
            eye("W3 b1")
            copy_a(2)
            for b in range(2, NB):
                eye(f"W3 b{b}")

        @block.scalar
        def _(act):
            def hi(dst, src):
                return nc.scalar.activation(dst, src, ACT.Copy)

            def w_hi_part(name):
                act.wait_ge(eye_added, w_count(name))
                wait_w_set(act, name)
                hi(w_hi[w_set(name)][:, :, :].rearrange("p k n -> p (k n)"), raw[:, slot(name), :])\
                    .then_inc(w_hi_made, 1)

            def a_part(n):
                act.wait_ge(a_in, 16 * NB * n)
                if n == 2:
                    act.wait_ge(low_done, low_count(1, PAIRS - 1))
                for pair in range(PAIRS):
                    ins = hi(a_group(pair, 0), a_pair(a_raw, pair))
                ins.then_inc(a_hi_made, 1)

            def b_part(n):
                act.wait_ge(raw_in[slot(f"B{n}")], raw_value(f"B{n}"))
                hi(b_stat[n - 1][:, :, :].rearrange("p q n -> p (q n)"), raw[:, slot(f"B{n}"), :])\
                    .then_inc(b_hi_made, 1)

            def drain(layer, g, m):
                act.wait_ge(acc_done, bank_no(layer, g, m) + 1)
                dst = x_hi[(layer + 1) % 2][:, m, group_cols(g)]
                if layer == 0:
                    ins = hi(dst, acc[m][:, :])
                else:
                    ins = nc.scalar.activation(dst, acc[m][:, :], ACT.Identity, bias=bias[:, layer - 1, m:m + 1])
                ins.then_inc(acc_hi_made, 1)

            low0 = raw[:, slot("low0"), :]
            act.wait_ge(low0_in[0], 16)
            hi(a0_hi[:, :, :].rearrange("p k n -> p (k n)"), low0[:, 0:NK * P])
            hi(router[:, :, 0:NE], low0[:, NK * P:NK * (P + NE)].rearrange("p (k e) -> p k e", k=NK))\
                .then_inc(low0_hi_made, 1)
            for k in range(NK):
                act.wait_ge(x0_in[k], 16)
                hi(x_hi[0][:, k, 0:GT], raw[:, slot("x g0"), k * GT:(k + 1) * GT]).then_inc(x_hi_made, 1)
            for k in range(NK):
                act.wait_ge(eye_added, k + 1)
                hi(w_hi[0][:, k, :], raw[:, slot("W0"), k * D:(k + 1) * D]).then_inc(w_hi_made, 1)
            act.wait_ge(low0_in[1], 16)
            hi(b0_hi[:, :], low0[:, NK * (P + NE):NK * (P + NE) + D]).then_inc(low0_hi_made, 1)

            def gate(g):
                act.wait_ge(shifted_made, g + 1)
                nc.scalar.activation(expd[:, :, :], shifted[:, :, :], ACT.Exp).then_inc(exp_done, 1)
                act.wait_ge(gates_made, g + 1)
                if g:
                    act.wait_ge(gates_turned, g)
                nc.scalar.activation(gate_wide,
                                     gates[:, :, :].unsqueeze(3).to_broadcast([P, GB, NE, R]),
                                     ACT.Copy).then_inc(gates_widened, 1)

            def gate_ranks(g):
                act.wait_ge(gates_turned, g + 1)
                if g:
                    act.wait_ge(gated_made, g)
                hi(gate_t, gate_ps[:, :]).then_inc(gates_copied, 1)
                act.wait_ge(gated_made, g + 1)
                if g:
                    act.wait_ge(acc_done, NK)
                hi(ranks[:, 0, :], gated).then_inc(ranks_hi_made, 1)

            gate(0)
            act.wait_ge(raw_in[slot("x g1")], raw_value("x g1"))
            gate_ranks(0)
            hi(x_hi[0][:, :, group_cols(1)], raw[:, slot("x g1"), :].rearrange("p (k t) -> p k t", k=NK))\
                .then_inc(x_hi_made, 1)
            a_part(1)
            b_part(1)
            w_hi_part("W1")
            for m in range(NK):
                drain(0, 0, m)
            gate(1)
            w_hi_part("W2")
            gate_ranks(1)
            b_part(2)
            for m in range(NK):
                drain(0, 1, m)

            def pair_ranks(layer, pair):
                act.wait_ge(low_done, low_count(layer, pair))
                if layer == 1 and pair == 0:
                    act.wait_ge(masks_made, 1)
                    act.wait_ge(acc_done, bank_no(1, 0, 0))
                mask = own_scaled if layer == 1 else own
                g, q = divmod(pair, 2)
                for side in range(2):
                    b = 2 * pair + side
                    ins = nc.scalar.activation(
                        ranks[:, g, q * PT + side * T:q * PT + (side + 1) * T],
                        low[q][:, side * T:(side + 1) * T], ACT.Copy, scale=mask[:, b:b + 1])
                ins.then_inc(ranks_hi_made, 1)

            for layer in (1, 2):
                for g in range(NG):
                    pair_ranks(layer, 2 * g)
                    pair_ranks(layer, 2 * g + 1)
                    for m in range(NK):
                        drain(layer, g, m)
                        if (layer, g, m) == (1, 0, 1):
                            w_hi_part("W3 b0")
                        if (layer, g, m) == (1, 1, 0):
                            a_part(2)
                        if (layer, g, m) == (1, 1, 1):
                            w_hi_part("W3 b1")
                        if (layer, g, m) == (2, 0, 1):
                            w_hi_part("W3 b2")
            w_hi_part("W3 b3")
            for b in range(NB):
                if b + 4 < NB:
                    w_hi_part(f"W3 b{b + 4}")
                if b % 2 == 0:
                    act.wait_ge(acc_done, bank_no_l3(b) + 1)
                    if b >= STAGES:
                        act.wait_ge(stored[b % STAGES], 16 * (b // STAGES))
                    nc.scalar.activation(stage[:, b % STAGES, :], acc[b % 4][:, :], ACT.Copy)\
                        .then_inc(out_read_act, 1)

        @block.vector
        def _(dve):
            steps = [0]

            def step(ins):
                steps[0] += 1
                ins.then_inc(dve_step, 1)
                dve.wait_ge(dve_step, steps[0])

            def lo(dst, src, hi_part):
                return nc.vector.tensor_tensor(dst, src, hi_part.bitcast(F32), ALU.subtract)

            def w_lo_part(name):
                dve.wait_ge(w_hi_made, w_count(name))
                s = w_set(name)
                lo(w_lo[s][:, :, :].rearrange("p k n -> p (k n)"), raw[:, slot(name), :],
                   w_hi[s][:, :, :].rearrange("p k n -> p (k n)")).then_inc(w_made, 1)

            def a_part(n):
                dve.wait_ge(a_hi_made, n)
                for pair in range(PAIRS):
                    ins = lo(a_group(pair, 2), a_pair(a_raw, pair), a_group(pair, 0))
                ins.then_inc(a_made, 1)

            def b_part(n):
                dve.wait_ge(b_hi_made, n)
                rows = slice(3 * PW, 4 * PW)
                b_rows = b_stat[n - 1][rows, :, :].rearrange("p q n -> p (q n)")
                lo(b_rows, raw[rows, slot(f"B{n}"), :], b_rows).then_inc(b_made, 1)

            def drain(layer, g, m):
                dve.wait_ge(acc_hi_made, bank_no(layer, g, m) + 1)
                i = (layer + 1) % 2
                h = x_hi[i][:, m, group_cols(g)]
                dst = x_lo[i][:, m, group_cols(g)]
                if layer == 0:
                    ins = lo(dst, acc[m][:, :], h)
                else:
                    ins = nc.vector.scalar_tensor_tensor(out=dst, in0=acc[m][:, :], scalar=bias[:, layer - 1, m:m + 1],
                                                         in1=h.bitcast(F32), op0=ALU.add, op1=ALU.subtract)
                ins.then_inc(acc_read, 1)

            low0 = raw[:, slot("low0"), :]
            dve.wait_ge(low0_hi_made, 1)
            lo(a0_lo[:, :, :].rearrange("p k n -> p (k n)"), low0[:, 0:NK * P],
               a0_hi[:, :, :].rearrange("p k n -> p (k n)"))
            lo(router[:, :, NE:2 * NE], low0[:, NK * P:NK * (P + NE)].rearrange("p (k e) -> p k e", k=NK),
               router[:, :, 0:NE]).then_inc(low0_made, 1)
            for k in range(NK):
                dve.wait_ge(x_hi_made, k + 1)
                lo(x_lo[0][:, k, 0:GT], raw[:, slot("x g0"), k * GT:(k + 1) * GT], x_hi[0][:, k, 0:GT])\
                    .then_inc(x_made, 1)

            def w0_chunk(k):
                dve.wait_ge(w_hi_made, k + 1)
                lo(w_lo[0][:, k, :], raw[:, slot("W0"), k * D:(k + 1) * D], w_hi[0][:, k, :]).then_inc(w_made, 1)

            def gate_logits(g):
                dve.wait_ge(logits_done, g + 1)
                bs = slice(g * GB, (g + 1) * GB)
                ins = nc.vector.tensor_reduce(logits[:, :, :], logit_ps[:, bs, :, :].rearrange("p b s e -> p b e s"),
                                              AX_X, ALU.add)
                ins.then_inc(logits_read, 1)
                dve.wait_ge(logits_read, g + 1)
                step(nc.vector.tensor_tensor(logits[:, :, :], logits[:, :, :], lang[:, bs, :], ALU.add))
                step(nc.vector.tensor_reduce(top[:, :], logits[:, :, :], AX_X, ALU.max))
                nc.vector.tensor_tensor(shifted[:, :, :], logits[:, :, :],
                                        top[:, :].unsqueeze(2).to_broadcast([P, GB, NE]), ALU.subtract)\
                    .then_inc(shifted_made, 1)

            def gate_choice(g):
                full = [P, GB, NE, NE]
                l_j = logits[:, :, :].unsqueeze(2).to_broadcast(full)
                l_i = logits[:, :, :].unsqueeze(3).to_broadcast(full)
                nc.vector.tensor_tensor(beats, l_j, l_i, ALU.is_gt)
                step(nc.vector.tensor_tensor(ties, l_j, l_i, ALU.is_equal))
                step(nc.vector.tensor_tensor(ties, ties,
                                             tie.unsqueeze(1).to_broadcast(full), ALU.mult))
                step(nc.vector.tensor_tensor(beats, beats, ties, ALU.add))
                step(nc.vector.tensor_reduce(rank[:, :, :], beats, AX_X, ALU.add))
                dve.wait_ge(exp_done, g + 1)
                step(nc.vector.scalar_tensor_tensor(out=kept[:, :, :], in0=rank[:, :, :], scalar=2.0,
                                                    in1=expd[:, :, :], op0=ALU.is_lt, op1=ALU.mult))
                step(nc.vector.tensor_reduce(total[:, :], kept[:, :, :], AX_X, ALU.add))
                step(nc.vector.reciprocal(total[:, :], total[:, :]))
                if g:
                    dve.wait_ge(gates_widened, g)
                nc.vector.scalar_tensor_tensor(out=gates[:, :, :], in0=kept[:, :, :], scalar=SCALING,
                                               in1=total[:, :].unsqueeze(2).to_broadcast([P, GB, NE]),
                                               op0=ALU.mult, op1=ALU.mult).then_inc(gates_made, 1)

            def gate_ranks(g):
                dve.wait_ge(gates_copied, g + 1)
                if g:
                    dve.wait_ge(ranks_hi_made, g)
                nc.vector.tensor_tensor(gated, low[g][:, :], gate_t, ALU.mult).then_inc(gated_made, 1)
                dve.wait_ge(ranks_hi_made, g + 1)
                lo(ranks[:, 1, :], gated, ranks[:, 0, :]).then_inc(ranks_made, 1)

            def language_mask():
                dve.wait_ge(consts_in, 16)
                dve.wait_ge(small_in, 5 * 16)
                step(nc.vector.tensor_copy(ids_f[:, :, :], ids_all[:, :, :]))
                step(nc.vector.tensor_tensor(lang[:, :, :], ids_f[:, 0, :].unsqueeze(2).to_broadcast([P, NB, NE]),
                                             expert.unsqueeze(1).to_broadcast([P, NB, NE]), ALU.is_equal))
                step(nc.vector.tensor_scalar(lang[:, :, :], lang[:, :, :], LANG_BIAS, None, ALU.mult))

            def scale_mask():
                step(nc.vector.tensor_tensor(pick[:, :, :], ids_f[:, 1, :].unsqueeze(2).to_broadcast([P, NB, NE]),
                                             expert.unsqueeze(1).to_broadcast([P, NB, NE]), ALU.is_equal))
                step(nc.vector.tensor_tensor(pick[:, :, :], pick[:, :, :],
                                             scale_all[:, :].unsqueeze(1).to_broadcast([P, NB, NE]), ALU.mult))
                step(nc.vector.tensor_reduce(scale_b[:, :], pick[:, :, :], AX_X, ALU.add))
                nc.vector.tensor_tensor(own_scaled[:, :], scale_b[:, :], own, ALU.mult).then_inc(masks_made, 1)
                dve.wait_ge(masks_made, 1)

            w0_chunk(0)
            language_mask()
            w0_chunk(1)
            gate_logits(0)
            w0_chunk(2)
            w0_chunk(3)
            gate_choice(0)
            scale_mask()
            dve.wait_ge(low0_hi_made, 2)
            lo(b0_lo[:, :], low0[:, NK * (P + NE):NK * (P + NE) + D], b0_hi[:, :]).then_inc(low0_made, 1)
            gate_ranks(0)
            dve.wait_ge(x_hi_made, NK + 1)
            lo(x_lo[0][:, :, group_cols(1)], raw[:, slot("x g1"), :].rearrange("p (k t) -> p k t", k=NK),
               x_hi[0][:, :, group_cols(1)]).then_inc(x_made, 1)
            a_part(1)
            b_part(1)
            w_lo_part("W1")
            for m in range(NK):
                drain(0, 0, m)
            gate_logits(1)
            gate_choice(1)
            w_lo_part("W2")
            gate_ranks(1)
            b_part(2)
            for m in range(NK):
                drain(0, 1, m)

            def pair_ranks(layer, pair):
                dve.wait_ge(ranks_hi_made, low_count(layer, pair))
                mask = own_scaled if layer == 1 else own
                g, q = divmod(pair, 2)
                rows = slice(PW, 2 * PW)
                for side in range(2):
                    b = 2 * pair + side
                    cols = ranks[rows, g, q * PT + side * T:q * PT + (side + 1) * T]
                    ins = nc.vector.scalar_tensor_tensor(out=cols, in0=low[q][rows, side * T:(side + 1) * T],
                                                         scalar=mask[rows, b:b + 1], in1=cols.bitcast(F32),
                                                         op0=ALU.mult, op1=ALU.subtract)
                ins.then_inc(ranks_made, 1)

            for layer in (1, 2):
                for g in range(NG):
                    pair_ranks(layer, 2 * g)
                    pair_ranks(layer, 2 * g + 1)
                    for m in range(NK):
                        drain(layer, g, m)
                        if (layer, g, m) == (1, 0, 1):
                            w_lo_part("W3 b0")
                        if (layer, g, m) == (1, 1, 0):
                            a_part(2)
                        if (layer, g, m) == (1, 1, 1):
                            w_lo_part("W3 b1")
                        if (layer, g, m) == (2, 0, 1):
                            w_lo_part("W3 b2")
            w_lo_part("W3 b3")
            for b in range(NB):
                if b + 4 < NB:
                    w_lo_part(f"W3 b{b + 4}")
                if b % 2 == 1:
                    dve.wait_ge(acc_done, bank_no_l3(b) + 1)
                    if b >= STAGES:
                        dve.wait_ge(stored[b % STAGES], 16 * (b // STAGES))
                    nc.vector.tensor_copy(stage[:, b % STAGES, :], acc[b % 4][:, :]).then_inc(out_read_dve, 1)

        @block.tensor
        def _(pe):
            mm = nc.tensor.matmul

            def low0_products(g):
                cols = group_cols(g)
                if g:
                    pe.wait_ge(x_made, NK + 1)
                    pe.wait_ge(logits_read, g)
                for k in range(NK):
                    if g == 0:
                        pe.wait_ge(x_made, k + 1)
                        if k == 0:
                            pe.wait_ge(low0_made, 1)
                    for i, (a, x) in enumerate(((a0_hi, x_hi[0]), (a0_hi, x_lo[0]), (a0_lo, x_hi[0]))):
                        last = mm(low[g][:, :], a[:, k, :], x[:, k, cols],
                                  start=(k == 0 and i == 0), stop=(k == NK - 1 and i == 2))
                    if k == NK - 1:
                        last.then_inc(low_done, 1)
                    for j in range(GB):
                        b = g * GB + j
                        for i, x in enumerate((x_hi[0], x_lo[0])):
                            last = mm(logit_ps[:, b, :, :].rearrange("p s e -> p (s e)"),
                                      x[:, k, batch_cols(b)], router[:, k, :],
                                      start=(k == 0 and j == 0 and i == 0),
                                      stop=(k == NK - 1 and i == 1), skip_group_check=True)
                last.then_inc(logits_done, 1)

            def bank_free(n):
                if n < 4:
                    return
                old = n - 4
                if old < bank_no_l3(0):
                    pe.wait_ge(acc_read, old + 1)
                elif (old - bank_no_l3(0)) % 2:
                    pe.wait_ge(out_read_dve, (old - bank_no_l3(0)) // 2 + 1)
                else:
                    pe.wait_ge(out_read_act, (old - bank_no_l3(0)) // 2 + 1)

            def base(layer, g, m, k, start, stop=False):
                s, i, cols = layer % W_SETS, layer % 2, group_cols(g)
                out_cols = slice(m * P, (m + 1) * P)
                mm(acc[m][:, :], w_hi[s][:, k, out_cols], x_hi[i][:, k, cols], start=start, stop=False)
                mm(acc[m][:, :], w_hi[s][:, k, out_cols], x_lo[i][:, k, cols], start=False, stop=False)
                return mm(acc[m][:, :], w_lo[s][:, k, out_cols], x_hi[i][:, k, cols], start=False, stop=stop)

            for g in range(NG):
                low0_products(g)
                for k in range(NK):
                    if g == 0:
                        pe.wait_ge(w_made, k + 1)
                    if k == 2:
                        pe.wait_ge(gates_widened, g + 1)
                        if g:
                            pe.wait_ge(gates_copied, g)
                        for j in range(GB):
                            last = nc.tensor.transpose(gate_ps[:, j * T:(j + 1) * T],
                                                       gate_wide[:, j, :, :].rearrange("p e r -> p (e r)"), ident)
                        last.then_inc(gates_turned, 1)
                    for m in range(NK):
                        if k == 0:
                            bank_free(bank_no(0, g, m))
                        base(0, g, m, k, start=(k == 0))
                pe.wait_ge(ranks_made, g + 1)
                if g == 0:
                    pe.wait_ge(low0_made, 2)
                for m in range(NK):
                    out_cols = slice(m * P, (m + 1) * P)
                    mm(acc[m][:, :], b0_hi[:, out_cols], ranks[:, 0, :], start=False, stop=False)
                    mm(acc[m][:, :], b0_hi[:, out_cols], ranks[:, 1, :], start=False, stop=False)
                    mm(acc[m][:, :], b0_lo[:, out_cols], ranks[:, 0, :], start=False, stop=True)\
                        .then_inc(acc_done, 1)

            for layer in (1, 2):
                pe.wait_ge(a_made, layer)
                pe.wait_ge(a_copied, layer)
                for g in range(NG):
                    i = layer % 2
                    for q in range(2):
                        pair = 2 * g + q
                        if q == 0:
                            pe.wait_ge(acc_read, bank_no(layer - 1, g, NK - 1) + 1)
                        if layer == 1 and g == 0:
                            pe.wait_ge(gated_made, q + 1)
                        else:
                            pe.wait_ge(ranks_made, low_count(layer, pair) - 2)
                        cols = slice(pair * PT, (pair + 1) * PT)
                        for k in range(NK):
                            for x in (x_hi[i], x_lo[i]):
                                last = mm(low[q][:, 0:PT], a_stat[:, pair, k, :], x[:, k, cols],
                                          start=(k == 0 and x is x_hi[i]), stop=(k == NK - 1 and x is x_lo[i]))
                        last.then_inc(low_done, 1)
                    if g == 0:
                        pe.wait_ge(w_made, w_count(f"W{layer}"))
                        pe.wait_ge(b_made, layer)
                    for m in range(NK):
                        bank_free(bank_no(layer, g, m))
                        for k in range(NK):
                            base(layer, g, m, k, start=(k == 0))
                        for q in range(2):
                            pair = 2 * g + q
                            if m == 0:
                                pe.wait_ge(ranks_made, low_count(layer, pair))
                            last = mm(acc[m][:, q * PT:(q + 1) * PT],
                                      b_stat[layer - 1][:, pair, m * P:(m + 1) * P],
                                      ranks[:, g, q * PT:(q + 1) * PT], start=False, stop=(q == 1))
                        last.then_inc(acc_done, 1)

            for b in range(NB):
                s = w_set(f"W3 b{b}")
                if b % GB == 0:
                    pe.wait_ge(acc_read, bank_no(2, b // GB, NK - 1) + 1)
                pe.wait_ge(w_made, w_count(f"W3 b{b}"))
                bank_free(bank_no_l3(b))
                for k in range(NK):
                    xh, xl = x_hi[1][:, k, batch_cols(b)], x_lo[1][:, k, batch_cols(b)]
                    mm(acc[b % 4][:, :], xh, w_hi[s][:, k, :], start=(k == 0), stop=False)
                    mm(acc[b % 4][:, :], xh, w_lo[s][:, k, :], start=False, stop=False)
                    last = mm(acc[b % 4][:, :], xl, w_hi[s][:, k, :], start=False, stop=(k == NK - 1))
                last.then_inc(acc_done, 1)


def kernel(x, itok_B_0_7, itok_B_1_7, itok_B_6_15, itok_B_3_7, L0_cond_W, L0_cond_Wr, L0_cond_A, L0_cond_B,
           L1_cond_weight, L1_cond_bias, L1_cond_lora_a_weights, L1_cond_lora_b_weights,
           L1_cond_scaling_factors, L2_cond_base_weight, L2_cond_base_bias, L2_cond_lora_A_w,
           L2_cond_lora_B_w, L3_cond_weight):
    import numpy as np
    import concourse.bacc as bacc
    from concourse.bass_utils import run_bass_kernel_spmd

    def chunks(a):
        return a.reshape(NK, P, -1).transpose(1, 0, 2)

    arr = np.asarray
    w0, w1, w2, w3 = (arr(a) for a in (L0_cond_W, L1_cond_weight, L2_cond_base_weight, L3_cond_weight))
    a0, b0, wr = arr(L0_cond_A), arr(L0_cond_B), arr(L0_cond_Wr)
    x_all = chunks(arr(x).reshape(NB * T, D).T)
    part = np.arange(P)
    consts = np.concatenate([
        np.eye(P),
        np.tile(np.arange(NE), (P, 1)),
        np.tile((np.arange(NE)[None, :] < np.arange(NE)[:, None]).reshape(1, -1), (P, 1)),
        (part[:, None] // R) % 2 == np.arange(NB)[None, :] % 2,
    ], axis=1).astype(np.float32)
    arrays = {
        "x_t": x_all.reshape(P, NK, NG, GT).transpose(2, 0, 1, 3),
        "w_t": np.stack([chunks(w.T) for w in (w0, w1, w2)]),
        "w3_t": np.stack([chunks(w.T) for w in w3]),
        "a0_t": np.concatenate([chunks(a0.reshape(NE * R, D).T).reshape(P, -1),
                                chunks(wr.T).reshape(P, -1)], axis=1),
        "b0_t": b0.transpose(0, 2, 1).reshape(NE * R, D),
        "a1_t": np.stack([chunks(a.T).reshape(P, -1) for a in arr(L1_cond_lora_a_weights)]),
        "b1_t": arr(L1_cond_lora_b_weights).transpose(0, 2, 1),
        "a2_t": np.stack([chunks(a.T).reshape(P, -1) for a in arr(L2_cond_lora_A_w)]),
        "b2_t": arr(L2_cond_lora_B_w).transpose(0, 2, 1),
        "bias1": arr(L1_cond_bias).reshape(NK, P).T,
        "bias2": arr(L2_cond_base_bias).reshape(NK, P).T,
        "scale1": arr(L1_cond_scaling_factors),
        "id0": arr(itok_B_0_7), "id1": arr(itok_B_1_7), "id2": arr(itok_B_6_15), "id3": arr(itok_B_3_7),
        "consts": consts,
    }
    arrays = {n: np.ascontiguousarray(a) for n, a in arrays.items()}
    nc = bacc.Bacc("TRN2", target_bir_lowering=False, num_devices=1)
    args = {n: nc.dram_tensor(n, a.shape, mybir.dt.from_np(a.dtype), kind="ExternalInput").ap()
            for n, a in arrays.items()}
    out = nc.dram_tensor("out", (NB, T, D), F32, kind="ExternalOutput").ap()
    build(nc, out=out, **args)
    r = run_bass_kernel_spmd(nc, [arrays], core_ids=[0])
    return r.results[0]["out"]
```

```python
from contextlib import ExitStack

import concourse.bass as bass
from concourse import mybir

F32 = mybir.dt.float32
F32R = mybir.dt.float32r
I32 = mybir.dt.int32
ALU = mybir.AluOpType
ACT = mybir.ActivationFunctionType
AX_X = mybir.AxisListType.X

P = 128
NB, T, D = 8, 128, 512
NK = D // P
NG = 2
GB = NB // NG
GT = GB * T
NE, R = 8, 16
N2 = 32
PAIRS = NB // 2
PW = 2 * R
PT = 2 * T
LANG_BIAS = 5.0
SCALING = 2.0

C_IDENT, C_EXPERT, C_TIE, C_OWN = 0, P, P + NE, P + NE + NE * NE
C_ALL = C_OWN + NB

RAW_SLOTS = 3
ENTRIES = ["x g0", "W0", "low0", "x g1", "W1", "B1", "W2", "B2"] + [f"W3 b{b}" for b in range(NB)]
W_SETS = 4
STAGES = 4
WARM_UP = 7


SPLIT_AFTER = {
    (1, 0, 0): ("W2", 0), (1, 0, 1): ("W2", 1), (1, 0, 2): ("B2", 0), (1, 0, 3): ("B2", 1),
    (1, 1, 0): ("A2", 0), (1, 1, 1): ("W3 b0", 0), (1, 1, 2): ("W3 b0", 1),
    (2, 0, 0): ("W3 b1", 0), (2, 0, 1): ("W3 b1", 1), (2, 0, 2): ("W3 b2", 0), (2, 0, 3): ("W3 b2", 1),
}


def entry(name):
    return ENTRIES.index(name)


def slot(name):
    return entry(name) % RAW_SLOTS


def loaded_before(name):
    return entry(name) // RAW_SLOTS


def build(nc, x_t, w_t, w3_t, a0_t, b0_t, a1_t, b1_t, a2_t, b2_t, bias1, bias2, scale1,
          id0, id1, id2, id3, consts, out):
    with ExitStack() as ctx:
        def sb(name, shape, dt):
            return ctx.enter_context(nc.sbuf_tensor(name, shape, dt))

        def ps(name, shape):
            return ctx.enter_context(nc.psum_tensor(name, shape, F32))

        def sem(name):
            return ctx.enter_context(nc.semaphore(name))

        raw = sb("raw", [P, RAW_SLOTS, NK * D], F32)
        x_hi = [sb(f"x_hi{i}", [P, NK, NB * T], F32R) for i in range(2)]
        x_lo = [sb(f"x_lo{i}", [P, NK, NB * T], F32R) for i in range(2)]
        w_hi = [sb(f"w_hi{i}", [P, NK, D], F32R) for i in range(W_SETS)]
        w_lo = [sb(f"w_lo{i}", [P, NK, D], F32R) for i in range(W_SETS)]
        a0_hi, a0_lo = sb("a0_hi", [P, NK, NE * R], F32R), sb("a0_lo", [P, NK, NE * R], F32R)
        b0_hi, b0_lo = sb("b0_hi", [P, D], F32R), sb("b0_lo", [P, D], F32R)
        router = sb("router", [P, NK, 2 * NE], F32R)
        a_raw = [sb(f"a_raw{i}", [P, NB, NK, R], F32) for i in range(2)]
        a_stat = sb("a_stat", [P, PAIRS, NK, P], F32R)
        b_stat = [sb(f"b_stat{i}", [P, PAIRS, D], F32R) for i in range(2)]
        ranks = sb("ranks", [P, 2, GT], F32R)
        stage = sb("stage", [P, STAGES, D], F32)
        beats, ties = (stage[:, 0, i * GB * NE * NE:(i + 1) * GB * NE * NE]
                       .rearrange("p (b i j) -> p b i j", b=GB, i=NE) for i in range(2))
        gate_t, gated = stage[:, 1, :], stage[:, 2, :]
        gate_wide = stage[:, 3, :].rearrange("p (b e r) -> p b e r", b=GB, e=NE)
        const = sb("const", [P, C_ALL], F32)
        ids = sb("ids", [1, 3, NB], I32)
        ids_all = sb("ids_all", [P, 2, NB], I32)
        ids_f = sb("ids_f", [P, 2, NB], F32)
        scale_all = sb("scale_all", [P, NE], F32)
        bias = sb("bias", [P, 2, NK], F32)
        lang = sb("lang", [P, NB, NE], F32)
        pick = sb("pick", [P, NB, NE], F32)
        scale_b = sb("scale_b", [P, NB], F32)
        own_scaled = sb("own_scaled", [P, NB], F32)
        logits = sb("logits", [P, GB, NE], F32)
        top = sb("top", [P, GB], F32)
        rank = sb("rank", [P, GB, NE], F32)
        shifted = sb("shifted", [P, GB, NE], F32)
        expd = sb("expd", [P, GB, NE], F32)
        logits_t = sb("logits_t", [2 * NE, GT], F32)
        kept = sb("kept", [P, GB, NE], F32)
        total = sb("total", [P, GB], F32)
        gates = sb("gates", [P, GB, NE], F32)

        ident = const[:, C_IDENT:C_IDENT + P]
        expert = const[:, C_EXPERT:C_EXPERT + NE]
        tie = const[:, C_TIE:C_TIE + NE * NE].rearrange("p (i j) -> p i j", i=NE)
        own = const[:, C_OWN:C_OWN + NB]

        zeros = w_lo[3][:, 0, :]

        acc = [ps(f"acc{i}", [P, D]) for i in range(4)]
        low = [ps(f"low{i}", [P, GT]) for i in range(2)]
        logit_ps = ps("logit_ps", [P, GT])
        gate_ps = ps("gate_ps", [P, GT])

        zeros_made = sem("zeros_made")
        consts_in = sem("consts_in")
        small_in = sem("small_in")
        ids_in = sem("ids_in")
        x0_in = [sem(f"x0_in{k}") for k in range(NK)]
        w0_in = [sem(f"w0_in{k}") for k in range(NK)]
        low0_in = [sem(f"low0_in{i}") for i in range(2)]
        raw_in = [sem(f"raw_in{i}") for i in range(RAW_SLOTS)]
        a_in = [sem(f"a_in{i}") for i in range(2)]
        masks_made = sem("masks_made")
        eye_added = sem("eye_added")
        w_hi_made = sem("w_hi_made")
        w_made = sem("w_made")
        x_hi_made = sem("x_hi_made")
        x_made = sem("x_made")
        low0_hi_made = sem("low0_hi_made")
        low0_made = sem("low0_made")
        a_hi_made = sem("a_hi_made")
        a_copied = sem("a_copied")
        a_made = sem("a_made")
        b_hi_made = sem("b_hi_made")
        b_copied = sem("b_copied")
        b_made = sem("b_made")
        logits_done = sem("logits_done")
        logits_copied = sem("logits_copied")
        logits_turned = sem("logits_turned")
        logits_read = sem("logits_read")
        dve_step = sem("dve_step")
        shifted_made = sem("shifted_made")
        exp_done = sem("exp_done")
        gates_made = sem("gates_made")
        gates_widened = sem("gates_widened")
        gates_turned = sem("gates_turned")
        gates_copied = sem("gates_copied")
        low_done = sem("low_done")
        gated_made = sem("gated_made")
        ranks_hi_made = sem("ranks_hi_made")
        ranks_made = sem("ranks_made")
        acc_done = sem("acc_done")
        acc_hi_made = sem("acc_hi_made")
        acc_read = sem("acc_read")
        out_read_act = sem("out_read_act")
        out_read_dve = sem("out_read_dve")
        stored = [sem(f"stored{i}") for i in range(STAGES)]

        W_ORDER = ["W0", "W1", "W2"] + [f"W3 b{b}" for b in range(NB)]

        def w_count(name, half=1):
            return NK + 2 * (W_ORDER.index(name) - 1) + half + 1 if name != "W0" else NK

        def w_set(name):
            return W_ORDER.index(name) % W_SETS

        def bank_no(layer, g, m):
            return (layer * NG + g) * NK + m

        def bank_no_l3(b):
            return 3 * NG * NK + b

        def low_count(layer, pair):
            return NG + (layer - 1) * PAIRS + pair + 1

        def batch_cols(b):
            return slice(b * T, (b + 1) * T)

        def group_cols(g):
            return slice(g * GT, (g + 1) * GT)

        def raw_value(name, half=False):
            dmas = {"x g0": 0, "W0": 0, "low0": 0, "B1": NB, "B2": NB}
            n = sum(dmas.get(e, 1) for i, e in enumerate(ENTRIES[:entry(name) + 1])
                    if i % RAW_SLOTS == slot(name))
            return 16 * n

        def flat_half(w, half):
            return w[:, 2 * half:2 * half + 2, :].rearrange("p k n -> p (k n)")

        def raw_half(name, half):
            return raw[:, slot(name), half * 2 * D:(half + 1) * 2 * D]

        def b_half(n, group, half):
            return b_stat[n - 1][group * PW:(group + 1) * PW, 2 * half:2 * half + 2, :]\
                .rearrange("p q n -> p (q n)")

        def a_pair(t, pair):
            return t[:, 2 * pair:2 * pair + 2, :, :].rearrange("p s k r -> p k s r")

        def a_group(pair, group):
            return a_stat[:, pair, :, group * PW:(group + 1) * PW].rearrange("p k (s r) -> p k s r", s=2)

        def wait_w_set(eng, name):
            n = W_ORDER.index(name) - W_SETS
            if n >= 0:
                last = bank_no(n, NG - 1, NK - 1) if n < 3 else bank_no_l3(n - 3)
                eng.wait_ge(acc_done, last + 1)

        block = ctx.enter_context(nc.Block())

        @block.sync
        def _(sp):
            def free_slot(name):
                e = entry(name) - RAW_SLOTS
                if e < 0:
                    return
                old = ENTRIES[e]
                if old == "x g0":
                    sp.wait_ge(x_made, NK)
                elif old == "x g1":
                    sp.wait_ge(x_made, NK + 1)
                elif old == "low0":
                    sp.wait_ge(low0_made, 2)
                elif old[0] == "B":
                    sp.wait_ge(b_made, 2 * int(old[1]))
                else:
                    sp.wait_ge(w_made, w_count(old))

            def load(name, src):
                free_slot(name)
                dst = raw[:, slot(name), :].rearrange("p (k n) -> p k n", k=NK)
                sp.dma_start(dst, src).then_inc(raw_in[slot(name)], 16)

            def gather(layer, a_dram, b_dram, n):
                free_slot(f"B{layer}")
                b_dst = raw[:, slot(f"B{layer}"), :].rearrange("p (q n) -> p q n", q=PAIRS)
                with sp.Fori(0, PAIRS) as q:
                    for side in range(2):
                        a = sp.value_load(ids[0:1, layer - 1, bass.ds(2 * q + side, 1)],
                                          min_val=0, max_val=n - 1)
                        sp.dma_start(a_raw[layer - 1][:, bass.ds(2 * q + side, 1), :, :]
                                     .rearrange("p b k r -> p (b k r)"),
                                     a_dram[bass.ds(a, 1)].rearrange("a p n -> p (a n)")).then_inc(a_in[layer - 1], 16)
                        sp.dma_start(b_dst[side * R:(side + 1) * R, bass.ds(q, 1), :].rearrange("p q n -> p (q n)"),
                                     b_dram[bass.ds(a, 1)].rearrange("a r n -> r (a n)"))\
                          .then_inc(raw_in[slot(f"B{layer}")], 16)

            low0 = raw[:, slot("low0"), :]
            sp.dma_start(low0[:, 0:NK * (P + NE)], a0_t).then_inc(low0_in[0], 16)
            for k in range(NK):
                sp.dma_start(raw[:, slot("x g0"), k * GT:(k + 1) * GT], x_t[0, :, k, :])\
                  .then_inc(x0_in[k], 16)
            sp.dma_start(const[:, :], consts).then_inc(consts_in, 16)
            for k in range(NK):
                sp.dma_start(raw[:, slot("W0"), k * D:(k + 1) * D], w_t[0, :, k, :]).then_inc(w0_in[k], 16)
            sp.dma_start(low0[:, NK * (P + NE):NK * (P + NE) + D], b0_t).then_inc(low0_in[1], 16)
            for i, src in enumerate((id1, id2, id3)):
                sp.dma_start(ids[:, i, :], src.rearrange("(a b) -> a b", a=1)).then_inc(ids_in, 16)
            load("x g1", x_t[1])
            load("W1", w_t[1])
            sp.wait_ge(ids_in, 3 * 16)
            gather(1, a1_t, b1_t, NE)
            load("W2", w_t[2])
            gather(2, a2_t, b2_t, N2)

            def load_w3(b):
                a = sp.value_load(ids[0:1, 2, b:b + 1], min_val=0, max_val=NE - 1)
                load(f"W3 b{b}", w3_t[bass.ds(a, 1)].rearrange("a p k n -> p (a k) n"))

            def store(b):
                sp.wait_ge(out_read_dve if b % 2 else out_read_act, b // 2 + 1)
                sp.dma_start(out[b], stage[:, b % STAGES, :]).then_inc(stored[b % STAGES], 16)

            for b in range(NB - 2):
                load_w3(b)
            load_w3(NB - 2)
            store(0)
            load_w3(NB - 1)
            for b in range(1, NB):
                store(b)
            for i in range(STAGES):
                sp.wait_ge(stored[i], 16 * (NB // STAGES))

        @block.gpsimd
        def _(pool):
            pool.dma_start(ids_all[:, 0, :], id0.rearrange("(a b) -> a b", a=1).to_broadcast([P, NB]))\
                .then_inc(small_in, 16)
            pool.dma_start(ids_all[:, 1, :], id1.rearrange("(a b) -> a b", a=1).to_broadcast([P, NB]))\
                .then_inc(small_in, 16)
            pool.dma_start(scale_all[:, :], scale1.rearrange("(a b) -> a b", a=1).to_broadcast([P, NE]))\
                .then_inc(small_in, 16)
            pool.dma_start(bias[:, 0, :], bias1).then_inc(small_in, 16)
            pool.dma_start(bias[:, 1, :], bias2).then_inc(small_in, 16)
            pool.wait_ge(consts_in, 16)

            def add_eye(name, k):
                block_k = raw[:, slot(name), k * (D + P):k * (D + P) + P]
                return nc.gpsimd.tensor_tensor(block_k, block_k, ident, ALU.add)

            for k in range(NK):
                pool.wait_ge(w0_in[k], 16)
                add_eye("W0", k).then_inc(eye_added, 1)

            def eye(name):
                pool.wait_ge(raw_in[slot(name)], raw_value(name))
                for half in range(2):
                    add_eye(name, 2 * half)
                    add_eye(name, 2 * half + 1).then_inc(eye_added, 1)

            def copy_a(n):
                pool.wait_ge(a_hi_made, n)
                sets = a_stat[:, :, :, :].rearrange("p q k m -> p (q k) m")
                for group in (1, 3):
                    ins = nc.gpsimd.tensor_copy(sets[:, :, group * PW:(group + 1) * PW],
                                                sets[:, :, 0:PW].bitcast(F32))
                ins.then_inc(a_copied, 1)

            def copy_b(n):
                pool.wait_ge(b_hi_made, 2 * n)
                for group in (1, 2):
                    pool.dma_start(b_stat[n - 1][group * PW:(group + 1) * PW, :, :].rearrange("p q n -> p (q n)"),
                                   b_stat[n - 1][0:PW, :, :].rearrange("p q n -> p (q n)")).then_inc(b_copied, 16)

            eye("W1")
            copy_a(1)
            copy_b(1)
            eye("W2")
            copy_b(2)
            copy_a(2)
            eye("W3 b0")
            eye("W3 b1")
            for b in range(2, NB):
                eye(f"W3 b{b}")

        @block.scalar
        def _(act):
            def hi(dst, src):
                return nc.scalar.activation(dst, src, ACT.Copy)

            def w_part(name, half):
                if half == 0:
                    wait_w_set(act, name)
                act.wait_ge(eye_added, w_count(name, half))
                hi(flat_half(w_hi[w_set(name)], half), raw_half(name, half)).then_inc(w_hi_made, 1)

            def a_part(n):
                act.wait_ge(a_in[n - 1], 16 * NB)
                if n == 2:
                    act.wait_ge(low_done, low_count(1, PAIRS - 1))
                for pair in range(PAIRS):
                    ins = hi(a_group(pair, 0), a_pair(a_raw[n - 1], pair))
                ins.then_inc(a_hi_made, 1)

            def b_part(n, half):
                act.wait_ge(raw_in[slot(f"B{n}")], raw_value(f"B{n}"))
                hi(b_half(n, 0, half), raw_half(f"B{n}", half)[0:PW, :]).then_inc(b_hi_made, 1)

            def drain(layer, g, m):
                act.wait_ge(acc_done, bank_no(layer, g, m) + 1)
                dst = x_hi[(layer + 1) % 2][:, m, group_cols(g)]
                if layer == 0:
                    ins = hi(dst, acc[m][:, :])
                else:
                    ins = nc.scalar.activation(dst, acc[m][:, :], ACT.Identity, bias=bias[:, layer - 1, m:m + 1])
                ins.then_inc(acc_hi_made, 1)

            def split(name, half):
                if name[0] == "W":
                    w_part(name, half)
                elif name[0] == "B":
                    b_part(int(name[1]), half)
                else:
                    a_part(int(name[1]))

            low0 = raw[:, slot("low0"), :]
            act.wait_ge(low0_in[0], 16)
            hi(a0_hi[:, :, :].rearrange("p k n -> p (k n)"), low0[:, 0:NK * P])
            hi(router[:, :, 0:NE], low0[:, NK * P:NK * (P + NE)].rearrange("p (k e) -> p k e", k=NK))\
                .then_inc(low0_hi_made, 1)
            for k in range(NK):
                act.wait_ge(x0_in[k], 16)
                hi(x_hi[0][:, k, 0:GT], raw[:, slot("x g0"), k * GT:(k + 1) * GT]).then_inc(x_hi_made, 1)
            for k in range(NK):
                act.wait_ge(eye_added, k + 1)
                hi(w_hi[0][:, k, :], raw[:, slot("W0"), k * D:(k + 1) * D]).then_inc(w_hi_made, 1)
            act.wait_ge(low0_in[1], 16)
            hi(b0_hi[:, :], low0[:, NK * (P + NE):NK * (P + NE) + D]).then_inc(low0_hi_made, 1)

            def copy_logits(g):
                act.wait_ge(logits_done, g + 1)
                if g:
                    act.wait_ge(logits_turned, g)
                hi(logits_t[:, :], logit_ps[0:2 * NE, :]).then_inc(logits_copied, 1)

            def gate(g):
                act.wait_ge(shifted_made, g + 1)
                nc.scalar.activation(expd[:, :, :], shifted[:, :, :], ACT.Exp).then_inc(exp_done, 1)
                act.wait_ge(gates_made, g + 1)
                if g:
                    act.wait_ge(gates_turned, g)
                nc.scalar.activation(gate_wide,
                                     gates[:, :, :].unsqueeze(3).to_broadcast([P, GB, NE, R]),
                                     ACT.Copy).then_inc(gates_widened, 1)

            def gate_ranks(g):
                act.wait_ge(gates_turned, g + 1)
                if g:
                    act.wait_ge(gated_made, g)
                hi(gate_t, gate_ps[:, :]).then_inc(gates_copied, 1)
                act.wait_ge(gated_made, g + 1)
                if g:
                    act.wait_ge(acc_done, NK)
                hi(ranks[:, 0, :], gated).then_inc(ranks_hi_made, 1)

            copy_logits(0)
            act.wait_ge(raw_in[slot("x g1")], raw_value("x g1"))
            hi(x_hi[0][:, :, group_cols(1)], raw[:, slot("x g1"), :].rearrange("p (k t) -> p k t", k=NK))\
                .then_inc(x_hi_made, 1)
            gate(0)
            gate_ranks(0)
            split("W1", 0)
            split("W1", 1)
            for m in range(NK):
                drain(0, 0, m)
            copy_logits(1)
            split("A1", 0)
            split("B1", 0)
            split("B1", 1)
            gate(1)
            gate_ranks(1)
            for m in range(NK):
                drain(0, 1, m)

            def pair_ranks(layer, pair):
                act.wait_ge(low_done, low_count(layer, pair))
                if layer == 1 and pair == 0:
                    act.wait_ge(masks_made, 1)
                    act.wait_ge(acc_done, bank_no(1, 0, 0))
                mask = own_scaled if layer == 1 else own
                g, q = divmod(pair, 2)
                for side in range(2):
                    b = 2 * pair + side
                    ins = nc.scalar.activation(
                        ranks[:, g, q * PT + side * T:q * PT + (side + 1) * T],
                        low[q][:, side * T:(side + 1) * T], ACT.Copy, scale=mask[:, b:b + 1])
                ins.then_inc(ranks_hi_made, 1)

            for layer in (1, 2):
                for g in range(NG):
                    pair_ranks(layer, 2 * g)
                    pair_ranks(layer, 2 * g + 1)
                    for m in range(NK):
                        drain(layer, g, m)
                        if (layer, g, m) in SPLIT_AFTER:
                            split(*SPLIT_AFTER[layer, g, m])
            for half in range(2):
                split("W3 b3", half)
            for b in range(NB):
                if b + 4 < NB:
                    for half in range(2):
                        split(f"W3 b{b + 4}", half)
                if b % 2 == 0:
                    act.wait_ge(acc_done, bank_no_l3(b) + 1)
                    if b >= STAGES:
                        act.wait_ge(stored[b % STAGES], 16 * (b // STAGES))
                    nc.scalar.activation(stage[:, b % STAGES, :], acc[b % 4][:, :], ACT.Copy)\
                        .then_inc(out_read_act, 1)

        @block.vector
        def _(dve):
            steps = [0]

            def step(ins):
                steps[0] += 1
                ins.then_inc(dve_step, 1)
                dve.wait_ge(dve_step, steps[0])

            def lo(dst, src, hi_part):
                return nc.vector.tensor_tensor(dst, src, hi_part.bitcast(F32), ALU.subtract)

            def w_part(name, half):
                dve.wait_ge(w_hi_made, w_count(name, half))
                lo(flat_half(w_lo[w_set(name)], half), raw_half(name, half),
                   flat_half(w_hi[w_set(name)], half)).then_inc(w_made, 1)

            def a_part(n):
                dve.wait_ge(a_hi_made, n)
                for pair in range(PAIRS):
                    ins = lo(a_group(pair, 2), a_pair(a_raw[n - 1], pair), a_group(pair, 0))
                ins.then_inc(a_made, 1)

            def b_part(n, half):
                dve.wait_ge(b_hi_made, 2 * (n - 1) + half + 1)
                lo(b_half(n, 3, half), raw_half(f"B{n}", half)[0:PW, :], b_half(n, 0, half)).then_inc(b_made, 1)

            def drain(layer, g, m):
                dve.wait_ge(acc_hi_made, bank_no(layer, g, m) + 1)
                i = (layer + 1) % 2
                h = x_hi[i][:, m, group_cols(g)]
                dst = x_lo[i][:, m, group_cols(g)]
                if layer == 0:
                    ins = lo(dst, acc[m][:, :], h)
                else:
                    ins = nc.vector.scalar_tensor_tensor(out=dst, in0=acc[m][:, :], scalar=bias[:, layer - 1, m:m + 1],
                                                         in1=h.bitcast(F32), op0=ALU.add, op1=ALU.subtract)
                ins.then_inc(acc_read, 1)

            def split(name, half):
                if name[0] == "W":
                    w_part(name, half)
                elif name[0] == "B":
                    b_part(int(name[1]), half)
                else:
                    a_part(int(name[1]))

            nc.vector.memset(zeros.bitcast(F32), 0.0).then_inc(zeros_made, 1)

            low0 = raw[:, slot("low0"), :]
            dve.wait_ge(low0_hi_made, 1)
            lo(a0_lo[:, :, :].rearrange("p k n -> p (k n)"), low0[:, 0:NK * P],
               a0_hi[:, :, :].rearrange("p k n -> p (k n)"))
            lo(router[:, :, NE:2 * NE], low0[:, NK * P:NK * (P + NE)].rearrange("p (k e) -> p k e", k=NK),
               router[:, :, 0:NE]).then_inc(low0_made, 1)
            for k in range(NK):
                dve.wait_ge(x_hi_made, k + 1)
                lo(x_lo[0][:, k, 0:GT], raw[:, slot("x g0"), k * GT:(k + 1) * GT], x_hi[0][:, k, 0:GT])\
                    .then_inc(x_made, 1)

            def w0_chunk(k):
                dve.wait_ge(w_hi_made, k + 1)
                lo(w_lo[0][:, k, :], raw[:, slot("W0"), k * D:(k + 1) * D], w_hi[0][:, k, :]).then_inc(w_made, 1)

            def gate_logits(g):
                dve.wait_ge(logits_turned, g + 1)
                bs = slice(g * GB, (g + 1) * GB)
                ins = nc.vector.tensor_reduce(logits[:, :, :], gate_ps[:, 0:GB * 2 * NE].rearrange("p (b s e) -> p b e s", b=GB, s=2),
                                              AX_X, ALU.add)
                ins.then_inc(logits_read, 1)
                dve.wait_ge(logits_read, g + 1)
                step(nc.vector.tensor_tensor(logits[:, :, :], logits[:, :, :], lang[:, bs, :], ALU.add))
                step(nc.vector.tensor_reduce(top[:, :], logits[:, :, :], AX_X, ALU.max))
                nc.vector.tensor_tensor(shifted[:, :, :], logits[:, :, :],
                                        top[:, :].unsqueeze(2).to_broadcast([P, GB, NE]), ALU.subtract)\
                    .then_inc(shifted_made, 1)

            def gate_choice(g):
                full = [P, GB, NE, NE]
                l_j = logits[:, :, :].unsqueeze(2).to_broadcast(full)
                l_i = logits[:, :, :].unsqueeze(3).to_broadcast(full)
                nc.vector.tensor_tensor(beats, l_j, l_i, ALU.is_gt)
                step(nc.vector.tensor_tensor(ties, l_j, l_i, ALU.is_equal))
                step(nc.vector.tensor_tensor(ties, ties,
                                             tie.unsqueeze(1).to_broadcast(full), ALU.mult))
                step(nc.vector.tensor_tensor(beats, beats, ties, ALU.add))
                step(nc.vector.tensor_reduce(rank[:, :, :], beats, AX_X, ALU.add))
                dve.wait_ge(exp_done, g + 1)
                step(nc.vector.scalar_tensor_tensor(out=kept[:, :, :], in0=rank[:, :, :], scalar=2.0,
                                                    in1=expd[:, :, :], op0=ALU.is_lt, op1=ALU.mult))
                step(nc.vector.tensor_reduce(total[:, :], kept[:, :, :], AX_X, ALU.add))
                step(nc.vector.reciprocal(total[:, :], total[:, :]))
                if g:
                    dve.wait_ge(gates_widened, g)
                nc.vector.scalar_tensor_tensor(out=gates[:, :, :], in0=kept[:, :, :], scalar=SCALING,
                                               in1=total[:, :].unsqueeze(2).to_broadcast([P, GB, NE]),
                                               op0=ALU.mult, op1=ALU.mult).then_inc(gates_made, 1)

            def gate_ranks(g):
                dve.wait_ge(gates_copied, g + 1)
                if g:
                    dve.wait_ge(ranks_hi_made, g)
                nc.vector.tensor_tensor(gated, low[g][:, :], gate_t, ALU.mult).then_inc(gated_made, 1)
                dve.wait_ge(ranks_hi_made, g + 1)
                lo(ranks[:, 1, :], gated, ranks[:, 0, :]).then_inc(ranks_made, 1)

            def language_mask():
                dve.wait_ge(consts_in, 16)
                dve.wait_ge(small_in, 5 * 16)
                step(nc.vector.tensor_copy(ids_f[:, :, :], ids_all[:, :, :]))
                step(nc.vector.tensor_tensor(lang[:, :, :], ids_f[:, 0, :].unsqueeze(2).to_broadcast([P, NB, NE]),
                                             expert.unsqueeze(1).to_broadcast([P, NB, NE]), ALU.is_equal))
                step(nc.vector.tensor_scalar(lang[:, :, :], lang[:, :, :], LANG_BIAS, None, ALU.mult))

            def scale_mask():
                step(nc.vector.tensor_tensor(pick[:, :, :], ids_f[:, 1, :].unsqueeze(2).to_broadcast([P, NB, NE]),
                                             expert.unsqueeze(1).to_broadcast([P, NB, NE]), ALU.is_equal))
                step(nc.vector.tensor_tensor(pick[:, :, :], pick[:, :, :],
                                             scale_all[:, :].unsqueeze(1).to_broadcast([P, NB, NE]), ALU.mult))
                step(nc.vector.tensor_reduce(scale_b[:, :], pick[:, :, :], AX_X, ALU.add))
                nc.vector.tensor_tensor(own_scaled[:, :], scale_b[:, :], own, ALU.mult).then_inc(masks_made, 1)
                dve.wait_ge(masks_made, 1)

            for k in range(NK):
                w0_chunk(k)
            dve.wait_ge(low0_hi_made, 2)
            lo(b0_lo[:, :], low0[:, NK * (P + NE):NK * (P + NE) + D], b0_hi[:, :]).then_inc(low0_made, 1)
            language_mask()
            scale_mask()
            gate_logits(0)
            gate_choice(0)
            gate_ranks(0)
            dve.wait_ge(x_hi_made, NK + 1)
            lo(x_lo[0][:, :, group_cols(1)], raw[:, slot("x g1"), :].rearrange("p (k t) -> p k t", k=NK),
               x_hi[0][:, :, group_cols(1)]).then_inc(x_made, 1)
            split("W1", 0)
            split("W1", 1)
            for m in range(NK):
                drain(0, 0, m)
            split("A1", 0)
            gate_logits(1)
            gate_choice(1)
            gate_ranks(1)
            split("B1", 0)
            split("B1", 1)
            for m in range(NK):
                drain(0, 1, m)

            def pair_ranks(layer, pair):
                dve.wait_ge(ranks_hi_made, low_count(layer, pair))
                mask = own_scaled if layer == 1 else own
                g, q = divmod(pair, 2)
                rows = slice(PW, 2 * PW)
                for side in range(2):
                    b = 2 * pair + side
                    cols = ranks[rows, g, q * PT + side * T:q * PT + (side + 1) * T]
                    ins = nc.vector.scalar_tensor_tensor(out=cols, in0=low[q][rows, side * T:(side + 1) * T],
                                                         scalar=mask[rows, b:b + 1], in1=cols.bitcast(F32),
                                                         op0=ALU.mult, op1=ALU.subtract)
                ins.then_inc(ranks_made, 1)

            for layer in (1, 2):
                for g in range(NG):
                    pair_ranks(layer, 2 * g)
                    pair_ranks(layer, 2 * g + 1)
                    for m in range(NK):
                        drain(layer, g, m)
                        if (layer, g, m) in SPLIT_AFTER:
                            split(*SPLIT_AFTER[layer, g, m])
            for half in range(2):
                split("W3 b3", half)
            for b in range(NB):
                if b + 4 < NB:
                    for half in range(2):
                        split(f"W3 b{b + 4}", half)
                if b % 2 == 1:
                    dve.wait_ge(acc_done, bank_no_l3(b) + 1)
                    if b >= STAGES:
                        dve.wait_ge(stored[b % STAGES], 16 * (b // STAGES))
                    nc.vector.tensor_copy(stage[:, b % STAGES, :], acc[b % 4][:, :]).then_inc(out_read_dve, 1)

        @block.tensor
        def _(pe):
            mm = nc.tensor.matmul

            pe.wait_ge(zeros_made, 1)
            for _ in range(WARM_UP):
                mm(acc[0][:, :], zeros[:, 0:P], zeros[:, :], start=True, stop=True)

            def low0_products(g):
                cols = group_cols(g)
                if g:
                    pe.wait_ge(x_made, NK + 1)
                    pe.wait_ge(logits_copied, g)
                for k in range(NK):
                    start, stop = k == 0, k == NK - 1
                    if g == 0:
                        pe.wait_ge(x_hi_made, k + 1)
                        pe.wait_ge(low0_hi_made, 1)
                    mm(low[g][:, :], a0_hi[:, k, :], x_hi[0][:, k, cols], start=start, stop=False)
                    if g == 0:
                        pe.wait_ge(low0_made, 1)
                    mm(low[g][:, :], a0_lo[:, k, :], x_hi[0][:, k, cols], start=False, stop=False)
                    mm(logit_ps[0:2 * NE, :], router[:, k, :], x_hi[0][:, k, cols], start=start, stop=False)
                    if g == 0:
                        pe.wait_ge(x_made, k + 1)
                    last = mm(logit_ps[0:2 * NE, :], router[:, k, :], x_lo[0][:, k, cols], start=False, stop=stop)
                    if stop:
                        last.then_inc(logits_done, 1)
                    last = mm(low[g][:, :], a0_hi[:, k, :], x_lo[0][:, k, cols], start=False, stop=stop)
                last.then_inc(low_done, 1)

            def turn_logits(g):
                pe.wait_ge(logits_copied, g + 1)
                if g:
                    pe.wait_ge(gates_copied, g)
                for j in range(GB):
                    last = nc.tensor.transpose(gate_ps[:, j * 2 * NE:(j + 1) * 2 * NE],
                                               logits_t[:, j * T:(j + 1) * T], ident[0:2 * NE, 0:2 * NE])
                last.then_inc(logits_turned, 1)

            def turn_gates(g):
                pe.wait_ge(gates_widened, g + 1)
                for j in range(GB):
                    last = nc.tensor.transpose(gate_ps[:, j * T:(j + 1) * T],
                                               gate_wide[:, j, :, :].rearrange("p e r -> p (e r)"), ident)
                last.then_inc(gates_turned, 1)

            def bank_free(n):
                if n < 4:
                    return
                old = n - 4
                if old < bank_no_l3(0):
                    pe.wait_ge(acc_read, old + 1)
                elif (old - bank_no_l3(0)) % 2:
                    pe.wait_ge(out_read_dve, (old - bank_no_l3(0)) // 2 + 1)
                else:
                    pe.wait_ge(out_read_act, (old - bank_no_l3(0)) // 2 + 1)

            def base(layer, g, m, k, start, stop=False):
                s, i, cols = layer % W_SETS, layer % 2, group_cols(g)
                out_cols = slice(m * P, (m + 1) * P)
                mm(acc[m][:, :], w_hi[s][:, k, out_cols], x_hi[i][:, k, cols], start=start, stop=False)
                mm(acc[m][:, :], w_hi[s][:, k, out_cols], x_lo[i][:, k, cols], start=False, stop=False)
                return mm(acc[m][:, :], w_lo[s][:, k, out_cols], x_hi[i][:, k, cols], start=False, stop=stop)

            for g in range(NG):
                low0_products(g)
                for k in range(NK):
                    if g == 0:
                        pe.wait_ge(w_made, k + 1)
                    if k == 1:
                        turn_logits(g)
                    for m in range(NK):
                        if k == 0:
                            bank_free(bank_no(0, g, m))
                        if (k, m) == (NK - 2, NK - 1):
                            turn_gates(g)
                        base(0, g, m, k, start=(k == 0))
                pe.wait_ge(ranks_made, g + 1)
                if g == 0:
                    pe.wait_ge(low0_made, 2)
                for m in range(NK):
                    out_cols = slice(m * P, (m + 1) * P)
                    mm(acc[m][:, :], b0_hi[:, out_cols], ranks[:, 0, :], start=False, stop=False)
                    mm(acc[m][:, :], b0_hi[:, out_cols], ranks[:, 1, :], start=False, stop=False)
                    mm(acc[m][:, :], b0_lo[:, out_cols], ranks[:, 0, :], start=False, stop=True)\
                        .then_inc(acc_done, 1)

            for layer in (1, 2):
                pe.wait_ge(a_made, layer)
                pe.wait_ge(a_copied, layer)
                for g in range(NG):
                    i = layer % 2
                    for q in range(2):
                        pair = 2 * g + q
                        if q == 0:
                            pe.wait_ge(acc_read, bank_no(layer - 1, g, NK - 1) + 1)
                        if layer == 1 and g == 0:
                            pe.wait_ge(gated_made, q + 1)
                        else:
                            pe.wait_ge(ranks_made, low_count(layer, pair) - 2)
                        cols = slice(pair * PT, (pair + 1) * PT)
                        for k in range(NK):
                            for x in (x_hi[i], x_lo[i]):
                                last = mm(low[q][:, 0:PT], a_stat[:, pair, k, :], x[:, k, cols],
                                          start=(k == 0 and x is x_hi[i]), stop=(k == NK - 1 and x is x_lo[i]))
                        last.then_inc(low_done, 1)
                    if g == 0:
                        pe.wait_ge(w_made, w_count(f"W{layer}"))
                        pe.wait_ge(b_made, 2 * layer)
                        pe.wait_ge(b_copied, 32 * layer)
                    for m in range(NK):
                        bank_free(bank_no(layer, g, m))
                        for k in range(NK):
                            base(layer, g, m, k, start=(k == 0))
                        for q in range(2):
                            pair = 2 * g + q
                            if m == 0:
                                pe.wait_ge(ranks_made, low_count(layer, pair))
                            last = mm(acc[m][:, q * PT:(q + 1) * PT],
                                      b_stat[layer - 1][:, pair, m * P:(m + 1) * P],
                                      ranks[:, g, q * PT:(q + 1) * PT], start=False, stop=(q == 1))
                        last.then_inc(acc_done, 1)

            for b in range(NB):
                s = w_set(f"W3 b{b}")
                if b % GB == 0:
                    pe.wait_ge(acc_read, bank_no(2, b // GB, NK - 1) + 1)
                pe.wait_ge(w_made, w_count(f"W3 b{b}"))
                bank_free(bank_no_l3(b))
                for k in range(NK):
                    xh, xl = x_hi[1][:, k, batch_cols(b)], x_lo[1][:, k, batch_cols(b)]
                    mm(acc[b % 4][:, :], xh, w_hi[s][:, k, :], start=(k == 0), stop=False)
                    mm(acc[b % 4][:, :], xh, w_lo[s][:, k, :], start=False, stop=False)
                    last = mm(acc[b % 4][:, :], xl, w_hi[s][:, k, :], start=False, stop=(k == NK - 1))
                last.then_inc(acc_done, 1)


def kernel(x, itok_B_0_7, itok_B_1_7, itok_B_6_15, itok_B_3_7, L0_cond_W, L0_cond_Wr, L0_cond_A, L0_cond_B,
           L1_cond_weight, L1_cond_bias, L1_cond_lora_a_weights, L1_cond_lora_b_weights,
           L1_cond_scaling_factors, L2_cond_base_weight, L2_cond_base_bias, L2_cond_lora_A_w,
           L2_cond_lora_B_w, L3_cond_weight):
    import numpy as np
    import concourse.bacc as bacc
    from concourse.bass_utils import run_bass_kernel_spmd

    def chunks(a):
        return a.reshape(NK, P, -1).transpose(1, 0, 2)

    arr = np.asarray
    w0, w1, w2, w3 = (arr(a) for a in (L0_cond_W, L1_cond_weight, L2_cond_base_weight, L3_cond_weight))
    a0, b0, wr = arr(L0_cond_A), arr(L0_cond_B), arr(L0_cond_Wr)
    x_all = chunks(arr(x).reshape(NB * T, D).T)
    part = np.arange(P)
    consts = np.concatenate([
        np.eye(P),
        np.tile(np.arange(NE), (P, 1)),
        np.tile((np.arange(NE)[None, :] < np.arange(NE)[:, None]).reshape(1, -1), (P, 1)),
        (part[:, None] // R) % 2 == np.arange(NB)[None, :] % 2,
    ], axis=1).astype(np.float32)
    arrays = {
        "x_t": x_all.reshape(P, NK, NG, GT).transpose(2, 0, 1, 3),
        "w_t": np.stack([chunks(w.T) for w in (w0, w1, w2)]),
        "w3_t": np.stack([chunks(w.T) for w in w3]),
        "a0_t": np.concatenate([chunks(a0.reshape(NE * R, D).T).reshape(P, -1),
                                chunks(wr.T).reshape(P, -1)], axis=1),
        "b0_t": b0.transpose(0, 2, 1).reshape(NE * R, D),
        "a1_t": np.stack([chunks(a.T).reshape(P, -1) for a in arr(L1_cond_lora_a_weights)]),
        "b1_t": arr(L1_cond_lora_b_weights).transpose(0, 2, 1),
        "a2_t": np.stack([chunks(a.T).reshape(P, -1) for a in arr(L2_cond_lora_A_w)]),
        "b2_t": arr(L2_cond_lora_B_w).transpose(0, 2, 1),
        "bias1": arr(L1_cond_bias).reshape(NK, P).T,
        "bias2": arr(L2_cond_base_bias).reshape(NK, P).T,
        "scale1": arr(L1_cond_scaling_factors),
        "id0": arr(itok_B_0_7), "id1": arr(itok_B_1_7), "id2": arr(itok_B_6_15), "id3": arr(itok_B_3_7),
        "consts": consts,
    }
    arrays = {n: np.ascontiguousarray(a) for n, a in arrays.items()}
    nc = bacc.Bacc("TRN2", target_bir_lowering=False, num_devices=1)
    args = {n: nc.dram_tensor(n, a.shape, mybir.dt.from_np(a.dtype), kind="ExternalInput").ap()
            for n, a in arrays.items()}
    out = nc.dram_tensor("out", (NB, T, D), F32, kind="ExternalOutput").ap()
    build(nc, out=out, **args)
    r = run_bass_kernel_spmd(nc, [arrays], core_ids=[0])
    return r.results[0]["out"]
```

```python
from contextlib import ExitStack

import concourse.bass as bass
from concourse import mybir

F32 = mybir.dt.float32
F32R = mybir.dt.float32r
I32 = mybir.dt.int32
ALU = mybir.AluOpType
ACT = mybir.ActivationFunctionType
AX_X = mybir.AxisListType.X

P = 128
NB, T, D = 8, 128, 512
NK = D // P
NG = 2
GB = NB // NG
GT = GB * T
NE, R = 8, 16
N2 = 32
PAIRS = NB // 2
PW = 2 * R
PT = 2 * T
LANG_BIAS = 5.0
SCALING = 2.0

C_IDENT, C_EXPERT, C_TIE, C_OWN = 0, P, P + NE, P + NE + NE * NE
C_ALL = C_OWN + NB

RAW_SLOTS = 3
ENTRIES = ["x g0", "W0", "low0", "x g1", "B1", "W1", "W2", "B2"] + [f"W3 b{b}" for b in range(NB)]
W_SETS = 4
STAGES = 4
WARM_UP = 15
WARM_COLS = 256
TURN_GATES_AT = [(NK - 2, NK - 1), (NK - 2, 1)]


W_PLACE = {"W0": 0, "W1": 1, "W2": 2, "W3 b0": 3, "W3 b1": 0, "W3 b2": 1, "W3 b3": "x g0", "W3 b4": "x g1",
           "W3 b5": 2, "W3 b6": 3, "W3 b7": 0}
W_ORDER = list(W_PLACE)
SPLIT_AFTER = {
    (1, 0, 0): ("W2", 0), (1, 0, 1): ("W2", 1), (1, 0, 2): ("B2", 0), (1, 0, 3): ("B2", 1),
    (1, 1, 0): ("A2", 0), (1, 1, 1): ("W3 b0", 0), (1, 1, 2): ("W3 b0", 1),
    (2, 0, 0): ("W3 b1", 0), (2, 0, 1): ("W3 b1", 1), (2, 0, 2): ("W3 b2", 0), (2, 0, 3): ("W3 b2", 1),
    (2, 1, 0): ("W3 b3", 0), (2, 1, 1): ("W3 b3", 1),
}


def entry(name):
    return ENTRIES.index(name)


def slot(name):
    return entry(name) % RAW_SLOTS




def build(nc, x_t, w_t, w3_t, a0_t, b0_t, a1_t, b1_t, a2_t, b2_t, bias1, bias2, scale1,
          id0, id1, id2, id3, consts, out):
    with ExitStack() as ctx:
        def sb(name, shape, dt):
            return ctx.enter_context(nc.sbuf_tensor(name, shape, dt))

        def ps(name, shape):
            return ctx.enter_context(nc.psum_tensor(name, shape, F32))

        def sem(name):
            return ctx.enter_context(nc.semaphore(name))

        raw = sb("raw", [P, RAW_SLOTS, NK * D], F32)
        x_hi = [sb(f"x_hi{i}", [P, NK, NB * T], F32R) for i in range(2)]
        x_lo = [sb(f"x_lo{i}", [P, NK, NB * T], F32R) for i in range(2)]
        w_hi = [sb(f"w_hi{i}", [P, NK, D], F32R) for i in range(W_SETS)]
        w_lo = [sb(f"w_lo{i}", [P, NK, D], F32R) for i in range(W_SETS)]
        low0_stat = sb("low0_stat", [P, NK, 2 * (P + NE)], F32R)
        b0_hi, b0_lo = sb("b0_hi", [P, D], F32R), sb("b0_lo", [P, D], F32R)
        a_raw = [sb(f"a_raw{i}", [P, NB, NK, R], F32) for i in range(2)]
        a_stat = sb("a_stat", [P, PAIRS, NK, P], F32R)
        b_stat = [sb(f"b_stat{i}", [P, PAIRS, D], F32R) for i in range(2)]
        ranks = sb("ranks", [P, 2, GT], F32R)
        stage = sb("stage", [P, STAGES, D], F32)
        beats, ties = (stage[:, 0, i * GB * NE * NE:(i + 1) * GB * NE * NE]
                       .rearrange("p (b i j) -> p b i j", b=GB, i=NE) for i in range(2))
        gate_t, gated = stage[:, 1, :], stage[:, 2, :]
        gate_wide = stage[:, 3, :].rearrange("p (b e r) -> p b e r", b=GB, e=NE)
        const = sb("const", [P, C_ALL], F32)
        ids = sb("ids", [1, 3, NB], I32)
        ids_all = sb("ids_all", [P, 2, NB], I32)
        ids_f = sb("ids_f", [P, 2, NB], F32)
        scale_all = sb("scale_all", [P, NE], F32)
        bias = sb("bias", [P, 2, NK], F32)
        lang = sb("lang", [P, NB, NE], F32)
        pick = sb("pick", [P, NB, NE], F32)
        scale_b = sb("scale_b", [P, NB], F32)
        own_scaled = sb("own_scaled", [P, NB], F32)
        logits = sb("logits", [P, GB, NE], F32)
        top = sb("top", [P, GB], F32)
        rank = sb("rank", [P, GB, NE], F32)
        shifted = sb("shifted", [P, GB, NE], F32)
        expd = sb("expd", [P, GB, NE], F32)
        logits_t = sb("logits_t", [2 * NE, GT], F32)
        kept = sb("kept", [P, GB, NE], F32)
        total = sb("total", [P, GB], F32)
        gates = sb("gates", [P, GB, NE], F32)

        a0_hi, a0_lo = low0_stat[:, :, 0:P], low0_stat[:, :, P + 2 * NE:2 * (P + NE)]
        router = low0_stat[:, :, P:P + 2 * NE]
        ident = const[:, C_IDENT:C_IDENT + P]
        expert = const[:, C_EXPERT:C_EXPERT + NE]
        tie = const[:, C_TIE:C_TIE + NE * NE].rearrange("p (i j) -> p i j", i=NE)
        own = const[:, C_OWN:C_OWN + NB]

        zeros = w_lo[3][:, 0, 0:WARM_COLS]

        acc = [ps(f"acc{i}", [P, D]) for i in range(4)]
        low = [ps(f"low{i}", [P, GT]) for i in range(2)]
        logit_ps = ps("logit_ps", [P, GT])
        gate_ps = ps("gate_ps", [P, GT])

        zeros_made = sem("zeros_made")
        consts_in = sem("consts_in")
        small_in = sem("small_in")
        bias_in = sem("bias_in")
        ids_in = sem("ids_in")
        x0_in = [sem(f"x0_in{k}") for k in range(NK)]
        w0_in = [sem(f"w0_in{k}") for k in range(NK)]
        low0_in = [sem(f"low0_in{i}") for i in range(NK + 1)]
        raw_in = [sem(f"raw_in{i}") for i in range(RAW_SLOTS)]
        a_in = [sem(f"a_in{i}") for i in range(2)]
        masks_made = sem("masks_made")
        eye_added = sem("eye_added")
        w_hi_made = sem("w_hi_made")
        w_made = sem("w_made")
        x_hi_made = sem("x_hi_made")
        x_made = sem("x_made")
        low0_hi_made = sem("low0_hi_made")
        low0_made = sem("low0_made")
        a_hi_made = sem("a_hi_made")
        a_copied = sem("a_copied")
        a_made = sem("a_made")
        b_hi_made = sem("b_hi_made")
        b_copied = sem("b_copied")
        b_made = sem("b_made")
        logits_done = sem("logits_done")
        logits_copied = sem("logits_copied")
        logits_turned = sem("logits_turned")
        logits_read = sem("logits_read")
        dve_step = sem("dve_step")
        shifted_made = sem("shifted_made")
        exp_done = sem("exp_done")
        gates_made = sem("gates_made")
        gates_widened = sem("gates_widened")
        gates_turned = sem("gates_turned")
        gates_copied = sem("gates_copied")
        low_done = sem("low_done")
        gated_made = sem("gated_made")
        ranks_hi_made = sem("ranks_hi_made")
        ranks_made = sem("ranks_made")
        acc_done = sem("acc_done")
        acc_hi_made = sem("acc_hi_made")
        acc_read = sem("acc_read")
        out_read_act = sem("out_read_act")
        out_read_dve = sem("out_read_dve")
        stored = [sem(f"stored{i}") for i in range(STAGES)]

        def w_count(name, half=1):
            return NK + 2 * (W_ORDER.index(name) - 1) + half + 1 if name != "W0" else NK

        def w_tile(w, x, name):
            place = W_PLACE[name]
            if isinstance(place, int):
                return w[place][:, :, :]
            return x[0][:, :, group_cols(int(place[3]))]

        def bank_no(layer, g, m):
            return (layer * NG + g) * NK + m

        def bank_no_l3(b):
            return 3 * NG * NK + b

        def low_count(layer, pair):
            return NG + (layer - 1) * PAIRS + pair + 1

        def batch_cols(b):
            return slice(b * T, (b + 1) * T)

        def group_cols(g):
            return slice(g * GT, (g + 1) * GT)

        def raw_value(name, half=False):
            dmas = {"x g0": 0, "W0": 0, "low0": 0, "B1": NB, "B2": NB}
            n = sum(dmas.get(e, 1) for i, e in enumerate(ENTRIES[:entry(name) + 1])
                    if i % RAW_SLOTS == slot(name))
            return 16 * n

        def chunk_pair(w, half):
            return w[:, 2 * half:2 * half + 2, :]

        def raw_half(name, half):
            return raw[:, slot(name), half * 2 * D:(half + 1) * 2 * D].rearrange("p (k n) -> p k n", k=2)

        def b_half(n, group, half):
            return b_stat[n - 1][group * PW:(group + 1) * PW, 2 * half:2 * half + 2, :]

        def a_pair(t, pair):
            return t[:, 2 * pair:2 * pair + 2, :, :].rearrange("p s k r -> p k s r")

        def a_group(pair, group):
            return a_stat[:, pair, :, group * PW:(group + 1) * PW].rearrange("p k (s r) -> p k s r", s=2)

        def wait_w_place(eng, name):
            place = W_PLACE[name]
            if not isinstance(place, int):
                eng.wait_ge(acc_done, bank_no(2, int(place[3]), NK - 1) + 1)
                return
            before = [n for n in W_ORDER[:W_ORDER.index(name)] if W_PLACE[n] == place]
            if before:
                old = before[-1]
                last = bank_no_l3(int(old[4])) if old[:2] == "W3" else bank_no(int(old[1]), NG - 1, NK - 1)
                eng.wait_ge(acc_done, last + 1)

        block = ctx.enter_context(nc.Block())

        @block.sync
        def _(sp):
            def free_slot(name):
                e = entry(name) - RAW_SLOTS
                if e < 0:
                    return
                old = ENTRIES[e]
                if old == "x g0":
                    sp.wait_ge(x_made, NK)
                elif old == "x g1":
                    sp.wait_ge(x_made, NK + 1)
                elif old == "low0":
                    sp.wait_ge(low0_made, NK + 1)
                elif old[0] == "B":
                    sp.wait_ge(b_made, 2 * int(old[1]))
                else:
                    sp.wait_ge(w_made, w_count(old))

            def load(name, src):
                free_slot(name)
                dst = raw[:, slot(name), :].rearrange("p (k n) -> p k n", k=NK)
                sp.dma_start(dst, src).then_inc(raw_in[slot(name)], 16)

            def gather(layer, a_dram, b_dram, n):
                free_slot(f"B{layer}")
                b_dst = raw[:, slot(f"B{layer}"), :].rearrange("p (q n) -> p q n", q=PAIRS)
                with sp.Fori(0, PAIRS) as q:
                    for side in range(2):
                        a = sp.value_load(ids[0:1, layer - 1, bass.ds(2 * q + side, 1)],
                                          min_val=0, max_val=n - 1)
                        sp.dma_start(a_raw[layer - 1][:, bass.ds(2 * q + side, 1), :, :]
                                     .rearrange("p b k r -> p (b k r)"),
                                     a_dram[bass.ds(a, 1)].rearrange("a p n -> p (a n)")).then_inc(a_in[layer - 1], 16)
                        sp.dma_start(b_dst[side * R:(side + 1) * R, bass.ds(q, 1), :].rearrange("p q n -> p (q n)"),
                                     b_dram[bass.ds(a, 1)].rearrange("a r n -> r (a n)"))\
                          .then_inc(raw_in[slot(f"B{layer}")], 16)

            low0 = raw[:, slot("low0"), :]
            for k in range(NK):
                sp.dma_start(raw[:, slot("x g0"), k * GT:(k + 1) * GT], x_t[0, :, k, :])\
                  .then_inc(x0_in[k], 16)
                sp.dma_start(low0[:, k * (P + NE):(k + 1) * (P + NE)], a0_t[:, k, :]).then_inc(low0_in[k], 16)
            sp.dma_start(const[:, :], consts).then_inc(consts_in, 16)
            for k in range(NK):
                sp.dma_start(raw[:, slot("W0"), k * D:(k + 1) * D], w_t[0, :, k, :]).then_inc(w0_in[k], 16)
            sp.dma_start(low0[:, NK * (P + NE):NK * (P + NE) + D], b0_t).then_inc(low0_in[NK], 16)
            for i, src in enumerate((id1, id2, id3)):
                sp.dma_start(ids[:, i, :], src.rearrange("(a b) -> a b", a=1)).then_inc(ids_in, 16)
            load("x g1", x_t[1])
            sp.wait_ge(ids_in, 3 * 16)
            gather(1, a1_t, b1_t, NE)
            load("W1", w_t[1])
            load("W2", w_t[2])
            gather(2, a2_t, b2_t, N2)

            def load_w3(b):
                a = sp.value_load(ids[0:1, 2, b:b + 1], min_val=0, max_val=NE - 1)
                load(f"W3 b{b}", w3_t[bass.ds(a, 1)].rearrange("a p k n -> p (a k) n"))

            def store(b):
                sp.wait_ge(out_read_dve if b % 2 else out_read_act, b // 2 + 1)
                sp.dma_start(out[b], stage[:, b % STAGES, :]).then_inc(stored[b % STAGES], 16)

            for b in range(NB):
                load_w3(b)
            for b in range(NB - 1):
                store(b)
            for half, (staged, n) in enumerate(((out_read_act, NB // 2 + 1), (out_read_dve, NB // 2))):
                cols = slice(half * D // 2, (half + 1) * D // 2)
                sp.wait_ge(staged, n)
                sp.dma_start(out[NB - 1, :, cols], stage[:, STAGES - 1, cols]).then_inc(stored[STAGES - 1], 16)
            for i in range(STAGES):
                stores = NB // STAGES + (i == STAGES - 1)
                sp.wait_ge(stored[i], 16 * stores)

        @block.gpsimd
        def _(pool):
            pool.dma_start(ids_all[:, 0, :], id0.rearrange("(a b) -> a b", a=1).to_broadcast([P, NB]))\
                .then_inc(small_in, 16)
            pool.dma_start(ids_all[:, 1, :], id1.rearrange("(a b) -> a b", a=1).to_broadcast([P, NB]))\
                .then_inc(small_in, 16)
            pool.dma_start(scale_all[:, :], scale1.rearrange("(a b) -> a b", a=1).to_broadcast([P, NE]))\
                .then_inc(small_in, 16)
            pool.dma_start(bias[:, 0, :], bias1).then_inc(bias_in, 16)
            pool.dma_start(bias[:, 1, :], bias2).then_inc(bias_in, 16)
            pool.wait_ge(consts_in, 16)

            def add_eye(name, k):
                block_k = raw[:, slot(name), k * (D + P):k * (D + P) + P]
                return nc.gpsimd.tensor_tensor(block_k, block_k, ident, ALU.add)

            for k in range(NK):
                pool.wait_ge(w0_in[k], 16)
                add_eye("W0", k).then_inc(eye_added, 1)

            def eye(name):
                pool.wait_ge(raw_in[slot(name)], raw_value(name))
                for half in range(2):
                    add_eye(name, 2 * half)
                    add_eye(name, 2 * half + 1).then_inc(eye_added, 1)

            def copy_a(n):
                pool.wait_ge(a_hi_made, n)
                sets = a_stat[:, :, :, :].rearrange("p q k m -> p (q k) m")
                for group in (1, 3):
                    ins = nc.gpsimd.tensor_copy(sets[:, :, group * PW:(group + 1) * PW],
                                                sets[:, :, 0:PW].bitcast(F32))
                ins.then_inc(a_copied, 1)

            def copy_b(n):
                pool.wait_ge(b_hi_made, 2 * n)
                for group in (1, 2):
                    pool.dma_start(b_stat[n - 1][group * PW:(group + 1) * PW, :, :].rearrange("p q n -> p (q n)"),
                                   b_stat[n - 1][0:PW, :, :].rearrange("p q n -> p (q n)")).then_inc(b_copied, 16)

            copy_a(1)
            copy_b(1)
            eye("W1")
            eye("W2")
            copy_b(2)
            copy_a(2)
            eye("W3 b0")
            eye("W3 b1")
            for b in range(2, NB):
                eye(f"W3 b{b}")

        @block.scalar
        def _(act):
            def hi(dst, src):
                return nc.scalar.activation(dst, src, ACT.Copy)

            def w_part(name, half):
                if half == 0:
                    wait_w_place(act, name)
                act.wait_ge(eye_added, w_count(name, half))
                hi(chunk_pair(w_tile(w_hi, x_hi, name), half), raw_half(name, half)).then_inc(w_hi_made, 1)

            def a_part(n):
                act.wait_ge(a_in[n - 1], 16 * NB)
                if n == 2:
                    act.wait_ge(low_done, low_count(1, PAIRS - 1))
                for pair in range(PAIRS):
                    ins = hi(a_group(pair, 0), a_pair(a_raw[n - 1], pair))
                ins.then_inc(a_hi_made, 1)

            def b_part(n, half):
                act.wait_ge(raw_in[slot(f"B{n}")], raw_value(f"B{n}"))
                hi(b_half(n, 0, half), raw_half(f"B{n}", half)[0:PW, :, :]).then_inc(b_hi_made, 1)

            def drain(layer, g, m):
                act.wait_ge(acc_done, bank_no(layer, g, m) + 1)
                dst = x_hi[(layer + 1) % 2][:, m, group_cols(g)]
                if layer == 0:
                    ins = hi(dst, acc[m][:, :])
                else:
                    ins = nc.scalar.activation(dst, acc[m][:, :], ACT.Identity, bias=bias[:, layer - 1, m:m + 1])
                ins.then_inc(acc_hi_made, 1)

            def copy_logits(g):
                act.wait_ge(logits_done, g + 1)
                if g:
                    act.wait_ge(logits_turned, g)
                hi(logits_t[:, :], logit_ps[0:2 * NE, :]).then_inc(logits_copied, 1)

            def split(name, half):
                if name[0] == "W":
                    w_part(name, half)
                elif name[0] == "B":
                    b_part(int(name[1]), half)
                else:
                    a_part(int(name[1]))

            low0 = raw[:, slot("low0"), :]
            for k in range(NK):
                act.wait_ge(x0_in[k], 16)
                hi(x_hi[0][:, k, 0:GT], raw[:, slot("x g0"), k * GT:(k + 1) * GT]).then_inc(x_hi_made, 1)
                act.wait_ge(low0_in[k], 16)
                hi(low0_stat[:, k, 0:P + NE], low0[:, k * (P + NE):(k + 1) * (P + NE)]).then_inc(low0_hi_made, 1)
            for k in range(NK):
                if k == NK - 1:
                    copy_logits(0)
                act.wait_ge(eye_added, k + 1)
                hi(w_hi[0][:, k, :], raw[:, slot("W0"), k * D:(k + 1) * D]).then_inc(w_hi_made, 1)
            act.wait_ge(low0_in[NK], 16)
            hi(b0_hi[:, :], low0[:, NK * (P + NE):NK * (P + NE) + D]).then_inc(low0_hi_made, 1)

            def gate_exp(g):
                act.wait_ge(shifted_made, g + 1)
                nc.scalar.activation(expd[:, :, :], shifted[:, :, :], ACT.Exp).then_inc(exp_done, 1)

            def widen_gates(g):
                act.wait_ge(gates_made, g + 1)
                if g:
                    act.wait_ge(gates_turned, g)
                nc.scalar.activation(gate_wide,
                                     gates[:, :, :].unsqueeze(3).to_broadcast([P, GB, NE, R]),
                                     ACT.Copy).then_inc(gates_widened, 1)

            def copy_gates(g):
                act.wait_ge(gates_turned, g + 1)
                if g:
                    act.wait_ge(gated_made, g)
                hi(gate_t, gate_ps[:, :]).then_inc(gates_copied, 1)

            def ranks_hi(g):
                act.wait_ge(gated_made, g + 1)
                if g:
                    act.wait_ge(acc_done, NK)
                hi(ranks[:, 0, :], gated).then_inc(ranks_hi_made, 1)

            gate_exp(0)
            act.wait_ge(raw_in[slot("x g1")], raw_value("x g1"))
            hi(x_hi[0][:, :, group_cols(1)], raw[:, slot("x g1"), :].rearrange("p (k t) -> p k t", k=NK))\
                .then_inc(x_hi_made, 1)
            widen_gates(0)
            copy_gates(0)
            ranks_hi(0)
            for m in range(NK):
                drain(0, 0, m)
            copy_logits(1)
            gate_exp(1)
            split("A1", 0)
            widen_gates(1)
            split("B1", 0)
            copy_gates(1)
            split("B1", 1)
            ranks_hi(1)
            split("W1", 0)
            split("W1", 1)
            for m in range(NK):
                drain(0, 1, m)

            def pair_ranks(layer, pair):
                act.wait_ge(low_done, low_count(layer, pair))
                if layer == 1 and pair == 0:
                    act.wait_ge(masks_made, 1)
                    act.wait_ge(acc_done, bank_no(1, 0, 0))
                mask = own_scaled if layer == 1 else own
                g, q = divmod(pair, 2)
                for side in range(2):
                    b = 2 * pair + side
                    ins = nc.scalar.activation(
                        ranks[:, g, q * PT + side * T:q * PT + (side + 1) * T],
                        low[q][:, side * T:(side + 1) * T], ACT.Copy, scale=mask[:, b:b + 1])
                ins.then_inc(ranks_hi_made, 1)

            act.wait_ge(bias_in, 2 * 16)
            for layer in (1, 2):
                for g in range(NG):
                    pair_ranks(layer, 2 * g)
                    pair_ranks(layer, 2 * g + 1)
                    for m in range(NK):
                        drain(layer, g, m)
                        if (layer, g, m) in SPLIT_AFTER:
                            split(*SPLIT_AFTER[layer, g, m])
            for name in ("W3 b4", "W3 b5"):
                for half in range(2):
                    split(name, half)
            for b in range(NB):
                if b % 2 == 0:
                    act.wait_ge(acc_done, bank_no_l3(b) + 1)
                    if b >= STAGES:
                        act.wait_ge(stored[b % STAGES], 16 * (b // STAGES))
                    hi(stage[:, b % STAGES, :], acc[b % 4][:, :]).then_inc(out_read_act, 1)
                if b + 6 < NB:
                    for half in range(2):
                        split(f"W3 b{b + 6}", half)
            act.wait_ge(acc_done, bank_no_l3(NB - 1) + 1)
            act.wait_ge(stored[STAGES - 1], 16)
            hi(stage[:, STAGES - 1, 0:D // 2], acc[3][:, 0:D // 2]).then_inc(out_read_act, 1)

        @block.vector
        def _(dve):
            steps = [0]

            def step(ins):
                steps[0] += 1
                ins.then_inc(dve_step, 1)
                dve.wait_ge(dve_step, steps[0])

            def lo(dst, src, hi_part):
                return nc.vector.tensor_tensor(dst, src, hi_part.bitcast(F32), ALU.subtract)

            def w_part(name, half):
                dve.wait_ge(w_hi_made, w_count(name, half))
                lo(chunk_pair(w_tile(w_lo, x_lo, name), half), raw_half(name, half),
                   chunk_pair(w_tile(w_hi, x_hi, name), half)).then_inc(w_made, 1)

            def a_part(n):
                dve.wait_ge(a_hi_made, n)
                for pair in range(PAIRS):
                    ins = lo(a_group(pair, 2), a_pair(a_raw[n - 1], pair), a_group(pair, 0))
                ins.then_inc(a_made, 1)

            def b_part(n, half):
                dve.wait_ge(b_hi_made, 2 * (n - 1) + half + 1)
                lo(b_half(n, 3, half), raw_half(f"B{n}", half)[0:PW, :, :], b_half(n, 0, half)).then_inc(b_made, 1)

            def drain(layer, g, m):
                dve.wait_ge(acc_hi_made, bank_no(layer, g, m) + 1)
                i = (layer + 1) % 2
                h = x_hi[i][:, m, group_cols(g)]
                dst = x_lo[i][:, m, group_cols(g)]
                if layer == 0:
                    ins = lo(dst, acc[m][:, :], h)
                else:
                    ins = nc.vector.scalar_tensor_tensor(out=dst, in0=acc[m][:, :], scalar=bias[:, layer - 1, m:m + 1],
                                                         in1=h.bitcast(F32), op0=ALU.add, op1=ALU.subtract)
                ins.then_inc(acc_read, 1)

            def split(name, half):
                if name[0] == "W":
                    w_part(name, half)
                elif name[0] == "B":
                    b_part(int(name[1]), half)
                else:
                    a_part(int(name[1]))

            nc.vector.memset(zeros.bitcast(F32), 0.0).then_inc(zeros_made, 1)

            low0 = raw[:, slot("low0"), :]
            for k in range(NK):
                at = k * (P + NE)
                dve.wait_ge(low0_hi_made, k + 1)
                lo(a0_lo[:, k, :], low0[:, at:at + P], a0_hi[:, k, :])
                lo(router[:, k, NE:2 * NE], low0[:, at + P:at + P + NE], router[:, k, 0:NE]).then_inc(low0_made, 1)
                dve.wait_ge(x_hi_made, k + 1)
                lo(x_lo[0][:, k, 0:GT], raw[:, slot("x g0"), k * GT:(k + 1) * GT], x_hi[0][:, k, 0:GT])\
                    .then_inc(x_made, 1)

            def w0_chunk(k):
                dve.wait_ge(w_hi_made, k + 1)
                lo(w_lo[0][:, k, :], raw[:, slot("W0"), k * D:(k + 1) * D], w_hi[0][:, k, :]).then_inc(w_made, 1)

            def gate_logits(g):
                dve.wait_ge(logits_turned, g + 1)
                bs = slice(g * GB, (g + 1) * GB)
                ins = nc.vector.tensor_reduce(logits[:, :, :], gate_ps[:, 0:GB * 2 * NE].rearrange("p (b s e) -> p b e s", b=GB, s=2),
                                              AX_X, ALU.add)
                ins.then_inc(logits_read, 1)
                dve.wait_ge(logits_read, g + 1)
                step(nc.vector.tensor_tensor(logits[:, :, :], logits[:, :, :], lang[:, bs, :], ALU.add))
                step(nc.vector.tensor_reduce(top[:, :], logits[:, :, :], AX_X, ALU.max))
                nc.vector.tensor_tensor(shifted[:, :, :], logits[:, :, :],
                                        top[:, :].unsqueeze(2).to_broadcast([P, GB, NE]), ALU.subtract)\
                    .then_inc(shifted_made, 1)

            def gate_choice(g):
                full = [P, GB, NE, NE]
                l_j = logits[:, :, :].unsqueeze(2).to_broadcast(full)
                l_i = logits[:, :, :].unsqueeze(3).to_broadcast(full)
                nc.vector.tensor_tensor(beats, l_j, l_i, ALU.is_gt)
                step(nc.vector.tensor_tensor(ties, l_j, l_i, ALU.is_equal))
                step(nc.vector.tensor_tensor(ties, ties,
                                             tie.unsqueeze(1).to_broadcast(full), ALU.mult))
                step(nc.vector.tensor_tensor(beats, beats, ties, ALU.add))
                step(nc.vector.tensor_reduce(rank[:, :, :], beats, AX_X, ALU.add))
                dve.wait_ge(exp_done, g + 1)
                step(nc.vector.scalar_tensor_tensor(out=kept[:, :, :], in0=rank[:, :, :], scalar=2.0,
                                                    in1=expd[:, :, :], op0=ALU.is_lt, op1=ALU.mult))
                step(nc.vector.tensor_reduce(total[:, :], kept[:, :, :], AX_X, ALU.add))
                step(nc.vector.reciprocal(total[:, :], total[:, :]))
                if g:
                    dve.wait_ge(gates_widened, g)
                nc.vector.scalar_tensor_tensor(out=gates[:, :, :], in0=kept[:, :, :], scalar=SCALING,
                                               in1=total[:, :].unsqueeze(2).to_broadcast([P, GB, NE]),
                                               op0=ALU.mult, op1=ALU.mult).then_inc(gates_made, 1)

            def ranks_gated(g):
                dve.wait_ge(gates_copied, g + 1)
                if g:
                    dve.wait_ge(ranks_hi_made, g)
                nc.vector.tensor_tensor(gated, low[g][:, :], gate_t, ALU.mult).then_inc(gated_made, 1)

            def ranks_lo(g):
                dve.wait_ge(ranks_hi_made, g + 1)
                lo(ranks[:, 1, :], gated, ranks[:, 0, :]).then_inc(ranks_made, 1)

            def language_mask():
                dve.wait_ge(consts_in, 16)
                dve.wait_ge(small_in, 3 * 16)
                step(nc.vector.tensor_copy(ids_f[:, :, :], ids_all[:, :, :]))
                step(nc.vector.tensor_tensor(lang[:, :, :], ids_f[:, 0, :].unsqueeze(2).to_broadcast([P, NB, NE]),
                                             expert.unsqueeze(1).to_broadcast([P, NB, NE]), ALU.is_equal))
                step(nc.vector.tensor_scalar(lang[:, :, :], lang[:, :, :], LANG_BIAS, None, ALU.mult))

            def scale_mask():
                step(nc.vector.tensor_tensor(pick[:, :, :], ids_f[:, 1, :].unsqueeze(2).to_broadcast([P, NB, NE]),
                                             expert.unsqueeze(1).to_broadcast([P, NB, NE]), ALU.is_equal))
                step(nc.vector.tensor_tensor(pick[:, :, :], pick[:, :, :],
                                             scale_all[:, :].unsqueeze(1).to_broadcast([P, NB, NE]), ALU.mult))
                step(nc.vector.tensor_reduce(scale_b[:, :], pick[:, :, :], AX_X, ALU.add))
                nc.vector.tensor_tensor(own_scaled[:, :], scale_b[:, :], own, ALU.mult).then_inc(masks_made, 1)
                dve.wait_ge(masks_made, 1)

            w0_chunk(0)
            language_mask()
            scale_mask()
            w0_chunk(1)
            gate_logits(0)
            w0_chunk(2)
            w0_chunk(3)
            gate_choice(0)
            dve.wait_ge(low0_hi_made, NK + 1)
            lo(b0_lo[:, :], low0[:, NK * (P + NE):NK * (P + NE) + D], b0_hi[:, :]).then_inc(low0_made, 1)
            ranks_gated(0)
            ranks_lo(0)
            dve.wait_ge(x_hi_made, NK + 1)
            lo(x_lo[0][:, :, group_cols(1)], raw[:, slot("x g1"), :].rearrange("p (k t) -> p k t", k=NK),
               x_hi[0][:, :, group_cols(1)]).then_inc(x_made, 1)
            for m in range(NK):
                drain(0, 0, m)
            gate_logits(1)
            gate_choice(1)
            split("A1", 0)
            split("B1", 0)
            ranks_gated(1)
            split("B1", 1)
            ranks_lo(1)
            split("W1", 0)
            split("W1", 1)
            for m in range(NK):
                drain(0, 1, m)

            def pair_ranks(layer, pair):
                dve.wait_ge(ranks_hi_made, low_count(layer, pair))
                mask = own_scaled if layer == 1 else own
                g, q = divmod(pair, 2)
                rows = slice(PW, 2 * PW)
                for side in range(2):
                    b = 2 * pair + side
                    cols = ranks[rows, g, q * PT + side * T:q * PT + (side + 1) * T]
                    ins = nc.vector.scalar_tensor_tensor(out=cols, in0=low[q][rows, side * T:(side + 1) * T],
                                                         scalar=mask[rows, b:b + 1], in1=cols.bitcast(F32),
                                                         op0=ALU.mult, op1=ALU.subtract)
                ins.then_inc(ranks_made, 1)

            dve.wait_ge(bias_in, 2 * 16)
            for layer in (1, 2):
                for g in range(NG):
                    pair_ranks(layer, 2 * g)
                    pair_ranks(layer, 2 * g + 1)
                    for m in range(NK):
                        drain(layer, g, m)
                        if (layer, g, m) in SPLIT_AFTER:
                            split(*SPLIT_AFTER[layer, g, m])
            for name in ("W3 b4", "W3 b5"):
                for half in range(2):
                    split(name, half)
            for b in range(NB):
                if b % 2 == 1 and b < NB - 1:
                    dve.wait_ge(acc_done, bank_no_l3(b) + 1)
                    if b >= STAGES:
                        dve.wait_ge(stored[b % STAGES], 16 * (b // STAGES))
                    nc.vector.tensor_copy(stage[:, b % STAGES, :], acc[b % 4][:, :]).then_inc(out_read_dve, 1)
                if b + 6 < NB:
                    for half in range(2):
                        split(f"W3 b{b + 6}", half)
            dve.wait_ge(acc_done, bank_no_l3(NB - 1) + 2)
            dve.wait_ge(stored[STAGES - 1], 16)
            nc.vector.tensor_copy(stage[:, STAGES - 1, D // 2:D], acc[0][:, 0:D // 2]).then_inc(out_read_dve, 1)

        @block.tensor
        def _(pe):
            mm = nc.tensor.matmul

            pe.wait_ge(zeros_made, 1)
            for _ in range(WARM_UP):
                mm(acc[0][:, 0:WARM_COLS], zeros[:, 0:P], zeros, start=True, stop=True)

            def low0_products(g):
                cols = group_cols(g)
                if g:
                    pe.wait_ge(x_made, NK + 1)
                    pe.wait_ge(logits_copied, g)
                for k in range(NK):
                    start, stop = k == 0, k == NK - 1
                    if g == 0:
                        pe.wait_ge(x_hi_made, k + 1)
                        pe.wait_ge(low0_hi_made, k + 1)
                    mm(low[g][:, :], a0_hi[:, k, :], x_hi[0][:, k, cols], start=start, stop=False)
                    if g == 0:
                        pe.wait_ge(low0_made, k + 1)
                    mm(low[g][:, :], a0_lo[:, k, :], x_hi[0][:, k, cols], start=False, stop=False)
                    mm(logit_ps[0:2 * NE, :], router[:, k, :], x_hi[0][:, k, cols], start=start, stop=False)
                    if g == 0:
                        pe.wait_ge(x_made, k + 1)
                    last = mm(logit_ps[0:2 * NE, :], router[:, k, :], x_lo[0][:, k, cols], start=False, stop=stop)
                    if stop:
                        last.then_inc(logits_done, 1)
                    last = mm(low[g][:, :], a0_hi[:, k, :], x_lo[0][:, k, cols], start=False, stop=stop)
                last.then_inc(low_done, 1)

            def turn_logits(g):
                pe.wait_ge(logits_copied, g + 1)
                if g:
                    pe.wait_ge(gates_copied, g)
                for j in range(GB):
                    last = nc.tensor.transpose(gate_ps[:, j * 2 * NE:(j + 1) * 2 * NE],
                                               logits_t[:, j * T:(j + 1) * T], ident[0:2 * NE, 0:2 * NE])
                last.then_inc(logits_turned, 1)

            def turn_gates(g):
                pe.wait_ge(gates_widened, g + 1)
                for j in range(GB):
                    last = nc.tensor.transpose(gate_ps[:, j * T:(j + 1) * T],
                                               gate_wide[:, j, :, :].rearrange("p e r -> p (e r)"), ident)
                last.then_inc(gates_turned, 1)

            def bank_free(n):
                if n < 4:
                    return
                old = n - 4
                if old < bank_no_l3(0):
                    pe.wait_ge(acc_read, old + 1)
                elif (old - bank_no_l3(0)) % 2:
                    pe.wait_ge(out_read_dve, (old - bank_no_l3(0)) // 2 + 1)
                else:
                    pe.wait_ge(out_read_act, (old - bank_no_l3(0)) // 2 + 1)

            def base(layer, g, m, k, start, stop=False):
                s, i, cols = W_PLACE[f"W{layer}"], layer % 2, group_cols(g)
                out_cols = slice(m * P, (m + 1) * P)
                mm(acc[m][:, :], w_hi[s][:, k, out_cols], x_hi[i][:, k, cols], start=start, stop=False)
                mm(acc[m][:, :], w_hi[s][:, k, out_cols], x_lo[i][:, k, cols], start=False, stop=False)
                return mm(acc[m][:, :], w_lo[s][:, k, out_cols], x_hi[i][:, k, cols], start=False, stop=stop)

            for g in range(NG):
                low0_products(g)
                for k in range(NK):
                    if g == 0:
                        pe.wait_ge(w_made, k + 1)
                    for m in range(NK):
                        if k == 0:
                            bank_free(bank_no(0, g, m))
                        if (k, m) == (0, 2):
                            turn_logits(g)
                        if (k, m) == TURN_GATES_AT[g]:
                            turn_gates(g)
                        base(0, g, m, k, start=(k == 0))
                pe.wait_ge(ranks_made, g + 1)
                if g == 0:
                    pe.wait_ge(low0_made, NK + 1)
                for m in range(NK):
                    out_cols = slice(m * P, (m + 1) * P)
                    mm(acc[m][:, :], b0_hi[:, out_cols], ranks[:, 0, :], start=False, stop=False)
                    mm(acc[m][:, :], b0_hi[:, out_cols], ranks[:, 1, :], start=False, stop=False)
                    mm(acc[m][:, :], b0_lo[:, out_cols], ranks[:, 0, :], start=False, stop=True)\
                        .then_inc(acc_done, 1)

            def add_ranks(layer, g, m):
                if (g, m) == (0, 0):
                    pe.wait_ge(b_made, 2 * layer)
                    pe.wait_ge(b_copied, 32 * layer)
                for q in range(2):
                    pair = 2 * g + q
                    if m == 0:
                        pe.wait_ge(ranks_made, low_count(layer, pair))
                    last = mm(acc[m][:, q * PT:(q + 1) * PT],
                              b_stat[layer - 1][:, pair, m * P:(m + 1) * P],
                              ranks[:, g, q * PT:(q + 1) * PT], start=False, stop=(q == 1))
                last.then_inc(acc_done, 1)

            for layer in (1, 2):
                pe.wait_ge(a_made, layer)
                pe.wait_ge(a_copied, layer)
                for g in range(NG):
                    i = layer % 2
                    for q in range(2):
                        pair = 2 * g + q
                        if q == 0:
                            pe.wait_ge(acc_read, bank_no(layer - 1, g, NK - 1) + 1)
                        if layer == 1 and g == 0:
                            pe.wait_ge(gated_made, q + 1)
                        else:
                            pe.wait_ge(ranks_made, low_count(layer, pair) - 2)
                        cols = slice(pair * PT, (pair + 1) * PT)
                        for k in range(NK):
                            for x in (x_hi[i], x_lo[i]):
                                last = mm(low[q][:, 0:PT], a_stat[:, pair, k, :], x[:, k, cols],
                                          start=(k == 0 and x is x_hi[i]), stop=(k == NK - 1 and x is x_lo[i]))
                        last.then_inc(low_done, 1)
                    for m in range(NK):
                        bank_free(bank_no(layer, g, m))
                        for k in range(NK):
                            if (g, m) == (0, 0) and k % 2 == 0:
                                pe.wait_ge(w_made, w_count(f"W{layer}", k // 2))
                            base(layer, g, m, k, start=(k == 0))
                        for done in {0: (), 1: (0, 1)}.get(m, (m,)):
                            add_ranks(layer, g, done)

            for b in range(NB):
                wh, wl = (w_tile(w, x, f"W3 b{b}") for w, x in ((w_hi, x_hi), (w_lo, x_lo)))
                if b % GB == 0:
                    pe.wait_ge(acc_read, bank_no(2, b // GB, NK - 1) + 1)
                pe.wait_ge(w_made, w_count(f"W3 b{b}"))
                halves = 2 if b == NB - 1 else 1
                for half in range(halves):
                    bank_free(bank_no_l3(b) + half)
                    cols = slice(half * D // halves, (half + 1) * D // halves)
                    dst = acc[(b + half) % 4][:, 0:D // halves]
                    for k in range(NK):
                        xh, xl = x_hi[1][:, k, batch_cols(b)], x_lo[1][:, k, batch_cols(b)]
                        mm(dst, xh, wh[:, k, cols], start=(k == 0), stop=False)
                        mm(dst, xh, wl[:, k, cols], start=False, stop=False)
                        last = mm(dst, xl, wh[:, k, cols], start=False, stop=(k == NK - 1))
                    last.then_inc(acc_done, 1)


def kernel(x, itok_B_0_7, itok_B_1_7, itok_B_6_15, itok_B_3_7, L0_cond_W, L0_cond_Wr, L0_cond_A, L0_cond_B,
           L1_cond_weight, L1_cond_bias, L1_cond_lora_a_weights, L1_cond_lora_b_weights,
           L1_cond_scaling_factors, L2_cond_base_weight, L2_cond_base_bias, L2_cond_lora_A_w,
           L2_cond_lora_B_w, L3_cond_weight):
    import numpy as np
    import concourse.bacc as bacc
    from concourse.bass_utils import run_bass_kernel_spmd

    def chunks(a):
        return a.reshape(NK, P, -1).transpose(1, 0, 2)

    arr = np.asarray
    w0, w1, w2, w3 = (arr(a) for a in (L0_cond_W, L1_cond_weight, L2_cond_base_weight, L3_cond_weight))
    a0, b0, wr = arr(L0_cond_A), arr(L0_cond_B), arr(L0_cond_Wr)
    x_all = chunks(arr(x).reshape(NB * T, D).T)
    part = np.arange(P)
    consts = np.concatenate([
        np.eye(P),
        np.tile(np.arange(NE), (P, 1)),
        np.tile((np.arange(NE)[None, :] < np.arange(NE)[:, None]).reshape(1, -1), (P, 1)),
        (part[:, None] // R) % 2 == np.arange(NB)[None, :] % 2,
    ], axis=1).astype(np.float32)
    arrays = {
        "x_t": x_all.reshape(P, NK, NG, GT).transpose(2, 0, 1, 3),
        "w_t": np.stack([chunks(w.T) for w in (w0, w1, w2)]),
        "w3_t": np.stack([chunks(w.T) for w in w3]),
        "a0_t": np.concatenate([chunks(a0.reshape(NE * R, D).T), chunks(wr.T)], axis=2),
        "b0_t": b0.transpose(0, 2, 1).reshape(NE * R, D),
        "a1_t": np.stack([chunks(a.T).reshape(P, -1) for a in arr(L1_cond_lora_a_weights)]),
        "b1_t": arr(L1_cond_lora_b_weights).transpose(0, 2, 1),
        "a2_t": np.stack([chunks(a.T).reshape(P, -1) for a in arr(L2_cond_lora_A_w)]),
        "b2_t": arr(L2_cond_lora_B_w).transpose(0, 2, 1),
        "bias1": arr(L1_cond_bias).reshape(NK, P).T,
        "bias2": arr(L2_cond_base_bias).reshape(NK, P).T,
        "scale1": arr(L1_cond_scaling_factors),
        "id0": arr(itok_B_0_7), "id1": arr(itok_B_1_7), "id2": arr(itok_B_6_15), "id3": arr(itok_B_3_7),
        "consts": consts,
    }
    arrays = {n: np.ascontiguousarray(a) for n, a in arrays.items()}
    nc = bacc.Bacc("TRN2", target_bir_lowering=False, num_devices=1)
    args = {n: nc.dram_tensor(n, a.shape, mybir.dt.from_np(a.dtype), kind="ExternalInput").ap()
            for n, a in arrays.items()}
    out = nc.dram_tensor("out", (NB, T, D), F32, kind="ExternalOutput").ap()
    build(nc, out=out, **args)
    r = run_bass_kernel_spmd(nc, [arrays], core_ids=[0])
    return r.results[0]["out"]
```
